# Optimizing a Trainium2 kernel written in Bass

```python
import numpy as np
import jax
import jax.numpy as jnp

def _softmax(x, axis=-1):
    return jax.nn.softmax(x, axis=axis)

def _gelu(x):
    return jax.nn.gelu(x, approximate=True)

def _silu(x):
    return jax.nn.silu(x)

def _sigmoid(x):
    return jax.nn.sigmoid(x)

def _layernorm(x, axis=-1, eps=1e-05):
    m = jnp.mean(x, axis=axis, keepdims=True)
    v = jnp.var(x, axis=axis, keepdims=True)
    return (x - m) / jnp.sqrt(v + eps)

def _scatter_add(tgt, idx, src, axis=0):
    return tgt.at[idx].add(src)

def _segment_sum(src, seg, n):
    return jax.ops.segment_sum(src, seg, n)
kernel_name = 'mk_gnn_preln_d4_gnn_r16_e12ce8'

def setup_inputs(seed: int=0):
    np.random.seed(seed)
    _w = jnp.asarray

    def _rec_inputs():
        import jax
        import jax.numpy as jnp
        _gk = jax.random.key(seed)
        x = -0.0007083 + 1.001 * jax.random.normal(jax.random.fold_in(_gk, 1), (3125, 48), jnp.float32)
        src = jax.random.randint(jax.random.fold_in(_gk, 2), (100000,), 0, 3125, jnp.int32)
        dst = jnp.minimum((3125 * jax.random.uniform(jax.random.fold_in(_gk, 3), (100000,)) ** 2.0).astype(jnp.int32), 49999)
        _o = jnp.argsort(dst, stable=True)
        src = src[_o]
        dst = dst[_o]
        edge_attr_40 = jax.random.uniform(jax.random.fold_in(_gk, 13), (100000, 40), jnp.float32, 0.0, 1)
        edge_weight = jax.random.uniform(jax.random.fold_in(_gk, 15), (100000,), jnp.float32, 0.0, 7.99999)
        edge_weight1 = -0.000414295 + 0.999828 * jax.random.normal(jax.random.fold_in(_gk, 16), (100000, 1), jnp.float32)
        node_type_119 = jax.random.randint(jax.random.fold_in(_gk, 17), (3125,), 0, 119, jnp.int32)
        node_vec = jax.random.uniform(jax.random.fold_in(_gk, 18), (3125,), jnp.float32, 0.0, 3.99996)
        return (x, src, dst, edge_attr_40, edge_weight, edge_weight1, node_type_119, node_vec)
    x, src, dst, edge_attr_40, edge_weight, edge_weight1, node_type_119, node_vec = _rec_inputs()

    def _L0_gnn_setup():
        import jax, jax.numpy as jnp
        import numpy as np
        N = 3125
        E = 75000
        H = 48
        RBF = 40
        L = 4
        NELEM = 119
        G = 32
        CUT = 6.0

        def _ln(x, g, b):
            m = x.mean(-1, keepdims=True)
            v = ((x - m) ** 2).mean(-1, keepdims=True)
            return (x - m) * jax.lax.rsqrt(v + 1e-05) * g + b
        key = jax.random.key(seed)
        k = jax.random.split(key, 16)
        s = 0.1
        return {'h': jax.random.normal(k[0], (N, H), jnp.float32), 'edge_index': jax.random.randint(k[1], (2, E), 0, N), 'edge_attr': jax.random.uniform(k[2], (E, RBF), dtype=jnp.float32), 'distances': jax.random.uniform(k[3], (E,), dtype=jnp.float32) * 8.0, 'atom_z': jax.random.randint(k[4], (N,), 0, NELEM), 'node_mult': jax.random.uniform(k[5], (N,), dtype=jnp.float32) * 3.0 + 1.0, 'batch': jnp.sort(jax.random.randint(k[6], (N,), 0, 64)), 'Wq': jax.random.normal(k[7], (L, H, H), jnp.float32) * s, 'gq': jnp.ones((L, H), jnp.float32), 'bq': jnp.zeros((L, H), jnp.float32), 'Wk': jax.random.normal(k[8], (L, H, H), jnp.float32) * s, 'gk': jnp.ones((L, H), jnp.float32), 'bk': jnp.zeros((L, H), jnp.float32), 'Wm': jax.random.normal(k[9], (L, H, H), jnp.float32) * s, 'Wu': jax.random.normal(k[10], (L, 2 * H, H), jnp.float32) * s, 'go': jnp.ones((L, H), jnp.float32), 'bo': jnp.zeros((L, H), jnp.float32), 'F1W': jax.random.normal(k[11], (RBF, H), jnp.float32) * s, 'F1b': jnp.zeros((H,), jnp.float32), 'F2W': jax.random.normal(k[12], (H, H), jnp.float32) * s, 'F2b': jnp.zeros((H,), jnp.float32), 'gn': jnp.ones((H,), jnp.float32), 'bn': jnp.zeros((H,), jnp.float32), 'emb': jax.random.normal(k[13], (NELEM, G), jnp.float32) * 0.01, 'adapt': jax.random.normal(k[14], (G, G), jnp.float32) * 0.01}
    _L0_gnn_all = _L0_gnn_setup()
    _L0_gnn_in = {k: v for k, v in _L0_gnn_all.items() if k in ('Wq', 'gq', 'bq', 'Wk', 'gk', 'bk', 'Wm', 'Wu', 'go', 'bo', 'F1W', 'F1b', 'F2W', 'F2b', 'gn', 'bn', 'emb', 'adapt')}
    del _L0_gnn_all

    def _L1_gnn_setup():
        import jax, jax.numpy as jnp
        import numpy as np
        N_NODES = 6250
        N_EDGES = 100000
        N_CLASSES = 48
        key = jax.random.key(seed)
        k1, k2, k3, k4 = jax.random.split(key, 4)
        soft_label = jax.random.normal(k1, (N_NODES, N_CLASSES), dtype=jnp.float32)
        e = jax.random.normal(k2, (N_EDGES, 1), dtype=jnp.float32)
        src = jax.random.randint(k3, (N_EDGES,), 0, N_NODES)
        dst = jax.random.randint(k4, (N_EDGES,), 0, N_NODES)
        return {'soft_label': soft_label, 'e': e, 'src': src, 'dst': dst}
    _L1_gnn_all = _L1_gnn_setup()
    _L1_gnn_in = {k: v for k, v in _L1_gnn_all.items() if k in ()}
    del _L1_gnn_all

    def _L2_gnn_setup():
        import jax, jax.numpy as jnp
        import numpy as np
        N = 6250
        E = 100000
        D = 48
        K = 5
        ALPHA = 0.8
        key = jax.random.key(seed)
        k1, k2 = jax.random.split(key)
        x = jax.random.normal(k1, (N, D), dtype=jnp.float32)
        edge_index = jax.random.randint(k2, (2, E), 0, N, dtype=jnp.int32)
        return {'x': x, 'edge_index': edge_index}
    _L2_gnn_all = _L2_gnn_setup()
    _L2_gnn_in = {k: v for k, v in _L2_gnn_all.items() if k in ()}
    del _L2_gnn_all

    def _L3_gnn_setup():
        import math
        import jax, jax.numpy as jnp
        import numpy as np
        N, E, C, T = (3125, 50000, 48, 128)
        C3, C9 = (C * 3, C * 9)
        EPS = 1e-05

        def sinusoidal_emb(t, dim):
            half = dim // 2
            freqs = jnp.exp(jnp.arange(half, dtype=jnp.float32) * (-math.log(10000.0) / (half - 1)))
            ang = t[:, None] * freqs[None, :]
            return jnp.concatenate([jnp.sin(ang), jnp.cos(ang)], axis=-1)

        def gcn_conv(x, W, b, src, dst, n):
            h = x @ W
            loop = jnp.arange(n, dtype=src.dtype)
            s = jnp.concatenate([src, loop])
            d = jnp.concatenate([dst, loop])
            deg = jax.ops.segment_sum(jnp.ones_like(d, dtype=h.dtype), d, num_segments=n)
            dinv = jnp.where(deg > 0, jax.lax.rsqrt(deg), 0.0)
            norm = dinv[s] * dinv[d]
            out = jax.ops.segment_sum(h[s] * norm[:, None], d, num_segments=n)
            return out + b

        def batchnorm(x, g, b):
            mean = jnp.mean(x, axis=0)
            var = jnp.mean(jnp.square(x - mean), axis=0)
            return g * (x - mean) * jax.lax.rsqrt(var + EPS) + b
        key = jax.random.key(seed)
        ks = jax.random.split(key, 12)
        rn = lambda k, sh: jax.random.normal(k, sh, jnp.float32) * 0.05
        return {'x': jax.random.normal(ks[0], (N, C), jnp.float32), 'edge_index': jax.random.randint(ks[1], (2, E), 0, N, dtype=jnp.int32), 'timestep': jax.random.randint(ks[2], (1,), 0, 1000).astype(jnp.float32), 'Wtm': rn(ks[3], (T, T)), 'btm': jnp.zeros((T,), jnp.float32), 'W_in': rn(ks[4], (C, C3)), 'b_in': jnp.zeros((C3,), jnp.float32), 'g_in': jnp.ones((C3,), jnp.float32), 'be_in': jnp.zeros((C3,), jnp.float32), 'Wt1': rn(ks[5], (T, C9)), 'bt1': jnp.zeros((C9,), jnp.float32), 'Wc1': rn(ks[6], (C3, C9)), 'bc1': jnp.zeros((C9,), jnp.float32), 'g1': jnp.ones((C9,), jnp.float32), 'be1': jnp.zeros((C9,), jnp.float32), 'Wt2': rn(ks[7], (T, C3)), 'bt2': jnp.zeros((C3,), jnp.float32), 'Wc2': rn(ks[8], (C9, C3)), 'bc2': jnp.zeros((C3,), jnp.float32), 'g2': jnp.ones((C3,), jnp.float32), 'be2': jnp.zeros((C3,), jnp.float32), 'W_out': rn(ks[9], (C3, C)), 'b_out': jnp.zeros((C,), jnp.float32), 'g_out': jnp.ones((C,), jnp.float32), 'be_out': jnp.zeros((C,), jnp.float32)}
    _L3_gnn_all = _L3_gnn_setup()
    _L3_gnn_in = {k: v for k, v in _L3_gnn_all.items() if k in ('timestep', 'Wtm', 'btm', 'W_in', 'b_in', 'g_in', 'be_in', 'Wt1', 'bt1', 'Wc1', 'bc1', 'g1', 'be1', 'Wt2', 'bt2', 'Wc2', 'bc2', 'g2', 'be2', 'W_out', 'b_out', 'g_out', 'be_out')}
    del _L3_gnn_all
    return {'x': x, 'src': src, 'dst': dst, 'edge_attr_40': edge_attr_40, 'edge_weight': edge_weight, 'edge_weight1': edge_weight1, 'node_type_119': node_type_119, 'node_vec': node_vec, 'L0_gnn_Wq': _L0_gnn_in['Wq'], 'L0_gnn_gq': _L0_gnn_in['gq'], 'L0_gnn_bq': _L0_gnn_in['bq'], 'L0_gnn_Wk': _L0_gnn_in['Wk'], 'L0_gnn_gk': _L0_gnn_in['gk'], 'L0_gnn_bk': _L0_gnn_in['bk'], 'L0_gnn_Wm': _L0_gnn_in['Wm'], 'L0_gnn_Wu': _L0_gnn_in['Wu'], 'L0_gnn_go': _L0_gnn_in['go'], 'L0_gnn_bo': _L0_gnn_in['bo'], 'L0_gnn_F1W': _L0_gnn_in['F1W'], 'L0_gnn_F1b': _L0_gnn_in['F1b'], 'L0_gnn_F2W': _L0_gnn_in['F2W'], 'L0_gnn_F2b': _L0_gnn_in['F2b'], 'L0_gnn_gn': _L0_gnn_in['gn'], 'L0_gnn_bn': _L0_gnn_in['bn'], 'L0_gnn_emb': _L0_gnn_in['emb'], 'L0_gnn_adapt': _L0_gnn_in['adapt'], 'L3_gnn_timestep': _L3_gnn_in['timestep'], 'L3_gnn_Wtm': _L3_gnn_in['Wtm'], 'L3_gnn_btm': _L3_gnn_in['btm'], 'L3_gnn_W_in': _L3_gnn_in['W_in'], 'L3_gnn_b_in': _L3_gnn_in['b_in'], 'L3_gnn_g_in': _L3_gnn_in['g_in'], 'L3_gnn_be_in': _L3_gnn_in['be_in'], 'L3_gnn_Wt1': _L3_gnn_in['Wt1'], 'L3_gnn_bt1': _L3_gnn_in['bt1'], 'L3_gnn_Wc1': _L3_gnn_in['Wc1'], 'L3_gnn_bc1': _L3_gnn_in['bc1'], 'L3_gnn_g1': _L3_gnn_in['g1'], 'L3_gnn_be1': _L3_gnn_in['be1'], 'L3_gnn_Wt2': _L3_gnn_in['Wt2'], 'L3_gnn_bt2': _L3_gnn_in['bt2'], 'L3_gnn_Wc2': _L3_gnn_in['Wc2'], 'L3_gnn_bc2': _L3_gnn_in['bc2'], 'L3_gnn_g2': _L3_gnn_in['g2'], 'L3_gnn_be2': _L3_gnn_in['be2'], 'L3_gnn_W_out': _L3_gnn_in['W_out'], 'L3_gnn_b_out': _L3_gnn_in['b_out'], 'L3_gnn_g_out': _L3_gnn_in['g_out'], 'L3_gnn_be_out': _L3_gnn_in['be_out']}

def reference(x, src, dst, edge_attr_40, edge_weight, edge_weight1, node_type_119, node_vec, L0_gnn_Wq, L0_gnn_gq, L0_gnn_bq, L0_gnn_Wk, L0_gnn_gk, L0_gnn_bk, L0_gnn_Wm, L0_gnn_Wu, L0_gnn_go, L0_gnn_bo, L0_gnn_F1W, L0_gnn_F1b, L0_gnn_F2W, L0_gnn_F2b, L0_gnn_gn, L0_gnn_bn, L0_gnn_emb, L0_gnn_adapt, L3_gnn_timestep, L3_gnn_Wtm, L3_gnn_btm, L3_gnn_W_in, L3_gnn_b_in, L3_gnn_g_in, L3_gnn_be_in, L3_gnn_Wt1, L3_gnn_bt1, L3_gnn_Wc1, L3_gnn_bc1, L3_gnn_g1, L3_gnn_be1, L3_gnn_Wt2, L3_gnn_bt2, L3_gnn_Wc2, L3_gnn_bc2, L3_gnn_g2, L3_gnn_be2, L3_gnn_W_out, L3_gnn_b_out, L3_gnn_g_out, L3_gnn_be_out):
    import jax
    import jax.numpy as jnp

    def _L0_gnn_ref(h, edge_index, edge_attr, distances, atom_z, node_mult, batch, Wq, gq, bq, Wk, gk, bk, Wm, Wu, go, bo, F1W, F1b, F2W, F2b, gn, bn, emb, adapt):
        import jax, jax.numpy as jnp
        import numpy as np
        N = 3125
        E = 75000
        H = 48
        RBF = 40
        L = 4
        NELEM = 119
        G = 32
        CUT = 6.0

        def _ln(x, g, b):
            m = x.mean(-1, keepdims=True)
            v = ((x - m) ** 2).mean(-1, keepdims=True)
            return (x - m) * jax.lax.rsqrt(v + 1e-05) * g + b
        src, dst = (edge_index[0], edge_index[1])
        gate = jax.nn.silu(edge_attr @ F1W + F1b) @ F2W + F2b
        ei = emb[atom_z[src]]
        ej = emb[atom_z[dst]]
        gate = gate + (ei * (ej @ adapt)).sum(-1, keepdims=True)
        cw = jnp.where(distances < CUT, 0.5 * (jnp.cos(jnp.pi * distances / CUT) + 1.0), 0.0)
        mj = node_mult[dst]
        msg = gate * h[dst] * (cw * mj)[:, None]
        agg = jax.ops.segment_sum(msg, src, num_segments=N)
        tot = jnp.clip(jax.ops.segment_sum(mj, src, num_segments=N), 1e-08, None)
        h = _ln(h + agg / tot[:, None], gn, bn)
        logm = jnp.log(jnp.clip(node_mult, 1.0, None))
        for i in range(L):
            Q = _ln(h @ Wq[i], gq[i], bq[i])
            K = _ln(h @ Wk[i], gk[i], bk[i])
            qi = Q[src]
            kj = K[dst]
            score = (qi * kj).sum(-1) + 0.1 * (edge_attr * qi[:, :RBF]).sum(-1) + logm[dst]
            smax = jax.ops.segment_max(score, src, num_segments=N)
            es = jnp.exp(jnp.minimum(score - smax[src], 20.0))
            denom = jax.ops.segment_sum(es, src, num_segments=N)
            alpha = es / (denom[src] + 1e-10)
            m = h[dst] @ Wm[i]
            aggi = jax.ops.segment_sum(alpha[:, None] * m, src, num_segments=N)
            z = jnp.concatenate([h, aggi], axis=-1) @ Wu[i]
            z = jnp.where(z > 0, z, 0.01 * z)
            h = _ln(h + z, go[i], bo[i])
        return h

    def _L1_gnn_ref(soft_label, e, src, dst):
        import jax, jax.numpy as jnp
        import numpy as np
        N_NODES = 6250
        N_EDGES = 100000
        N_CLASSES = 48
        N = soft_label.shape[0]
        logits = e[:, 0]
        seg_max = jax.ops.segment_max(logits, dst, num_segments=N)
        seg_max = jnp.where(jnp.isfinite(seg_max), seg_max, 0.0)
        ex = jnp.exp(logits - seg_max[dst])
        seg_sum = jax.ops.segment_sum(ex, dst, num_segments=N)
        a = ex / seg_sum[dst]
        msg = soft_label[src] * a[:, None]
        rst = jax.ops.segment_sum(msg, dst, num_segments=N)
        return jax.nn.elu(rst)

    def _L2_gnn_ref(x, edge_index):
        import jax, jax.numpy as jnp
        import numpy as np
        N = 6250
        E = 100000
        D = 48
        K = 5
        ALPHA = 0.8
        n = x.shape[0]
        loops = jnp.arange(n, dtype=edge_index.dtype)
        row = jnp.concatenate([edge_index[0], loops])
        col = jnp.concatenate([edge_index[1], loops])
        deg = jax.ops.segment_sum(jnp.ones(row.shape, x.dtype), col, num_segments=n)
        dinv = jnp.where(deg > 0, jax.lax.rsqrt(deg), jnp.zeros((), x.dtype))
        w = dinv[row] * dinv[col]

        def step(h, _):
            m = jax.ops.segment_sum(w[:, None] * h[row], col, num_segments=n)
            h = (1.0 - ALPHA) * m + ALPHA * x
            return (h, None)
        h, _ = jax.lax.scan(step, x, None, length=K)
        return h

    def _L3_gnn_ref(x, edge_index, timestep, Wtm, btm, W_in, b_in, g_in, be_in, Wt1, bt1, Wc1, bc1, g1, be1, Wt2, bt2, Wc2, bc2, g2, be2, W_out, b_out, g_out, be_out):
        import math
        import jax, jax.numpy as jnp
        import numpy as np
        N, E, C, T = (3125, 50000, 48, 128)
        C3, C9 = (C * 3, C * 9)
        EPS = 1e-05

        def sinusoidal_emb(t, dim):
            half = dim // 2
            freqs = jnp.exp(jnp.arange(half, dtype=jnp.float32) * (-math.log(10000.0) / (half - 1)))
            ang = t[:, None] * freqs[None, :]
            return jnp.concatenate([jnp.sin(ang), jnp.cos(ang)], axis=-1)

        def gcn_conv(x, W, b, src, dst, n):
            h = x @ W
            loop = jnp.arange(n, dtype=src.dtype)
            s = jnp.concatenate([src, loop])
            d = jnp.concatenate([dst, loop])
            deg = jax.ops.segment_sum(jnp.ones_like(d, dtype=h.dtype), d, num_segments=n)
            dinv = jnp.where(deg > 0, jax.lax.rsqrt(deg), 0.0)
            norm = dinv[s] * dinv[d]
            out = jax.ops.segment_sum(h[s] * norm[:, None], d, num_segments=n)
            return out + b

        def batchnorm(x, g, b):
            mean = jnp.mean(x, axis=0)
            var = jnp.mean(jnp.square(x - mean), axis=0)
            return g * (x - mean) * jax.lax.rsqrt(var + EPS) + b
        src, dst = (edge_index[0], edge_index[1])
        n = x.shape[0]
        relu = jax.nn.relu
        t = relu(sinusoidal_emb(timestep, T) @ Wtm + btm)
        h = relu(batchnorm(gcn_conv(x, W_in, b_in, src, dst, n), g_in, be_in))
        te1 = relu(t @ Wt1 + bt1)
        h = batchnorm(relu(gcn_conv(h, Wc1, bc1, src, dst, n) + te1), g1, be1)
        te2 = relu(t @ Wt2 + bt2)
        h = batchnorm(relu(gcn_conv(h, Wc2, bc2, src, dst, n) + te2), g2, be2)
        return relu(batchnorm(gcn_conv(h, W_out, b_out, src, dst, n), g_out, be_out))
    edge_index = jnp.stack([src, dst])
    batch0 = jnp.zeros((3125,), jnp.int32)
    h = jnp.maximum(_layernorm(x, axis=-1), 0.0)
    x = x + _L0_gnn_ref(h, edge_index, edge_attr_40, edge_weight, node_type_119, node_vec, batch0, L0_gnn_Wq, L0_gnn_gq, L0_gnn_bq, L0_gnn_Wk, L0_gnn_gk, L0_gnn_bk, L0_gnn_Wm, L0_gnn_Wu, L0_gnn_go, L0_gnn_bo, L0_gnn_F1W, L0_gnn_F1b, L0_gnn_F2W, L0_gnn_F2b, L0_gnn_gn, L0_gnn_bn, L0_gnn_emb, L0_gnn_adapt)
    h = jnp.maximum(_layernorm(x, axis=-1), 0.0)
    x = x + _L1_gnn_ref(h, edge_weight1, src, dst)
    h = jnp.maximum(_layernorm(x, axis=-1), 0.0)
    x = x + _L2_gnn_ref(h, edge_index)
    h = jnp.maximum(_layernorm(x, axis=-1), 0.0)
    x = x + _L3_gnn_ref(h, edge_index, L3_gnn_timestep, L3_gnn_Wtm, L3_gnn_btm, L3_gnn_W_in, L3_gnn_b_in, L3_gnn_g_in, L3_gnn_be_in, L3_gnn_Wt1, L3_gnn_bt1, L3_gnn_Wc1, L3_gnn_bc1, L3_gnn_g1, L3_gnn_be1, L3_gnn_Wt2, L3_gnn_bt2, L3_gnn_Wc2, L3_gnn_bc2, L3_gnn_g2, L3_gnn_be2, L3_gnn_W_out, L3_gnn_b_out, L3_gnn_g_out, L3_gnn_be_out)
    return x

_drawn_inputs = setup_inputs


def setup_inputs(seed=0):
    import zlib

    import numpy as np

    out = dict(_drawn_inputs(seed))
    spreads = {'L0_gnn_gq': (1.0, 0.2),
     'L0_gnn_bq': (0.0, 0.1),
     'L0_gnn_gk': (1.0, 0.2),
     'L0_gnn_bk': (0.0, 2.0),
     'L0_gnn_go': (1.0, 0.2),
     'L0_gnn_bo': (0.0, 0.1),
     'L0_gnn_F1b': (0.0, 0.688),
     'L0_gnn_F2b': (0.0, 0.1),
     'L0_gnn_gn': (1.0, 0.2),
     'L0_gnn_bn': (0.0, 0.1),
     'L3_gnn_btm': (0.0, 0.1),
     'L3_gnn_b_in': (0.0, 2.0),
     'L3_gnn_g_in': (1.0, 0.2),
     'L3_gnn_be_in': (0.0, 0.1),
     'L3_gnn_bt1': (0.0, 0.1),
     'L3_gnn_bc1': (0.0, 0.1),
     'L3_gnn_g1': (1.0, 0.2),
     'L3_gnn_be1': (0.0, 0.1),
     'L3_gnn_bt2': (0.0, 0.1),
     'L3_gnn_bc2': (0.0, 0.1),
     'L3_gnn_g2': (1.0, 0.2),
     'L3_gnn_be2': (0.0, 0.1),
     'L3_gnn_b_out': (0.0, 2.0),
     'L3_gnn_g_out': (1.0, 0.2),
     'L3_gnn_be_out': (0.0, 0.377)}
    factors = {'L0_gnn_emb': 64.0, 'L0_gnn_adapt': 64.0}
    for name, (base, spread) in spreads.items():
        noise = np.random.default_rng([zlib.crc32(name.encode()), seed]).standard_normal(out[name].shape)
        drawn = base * np.exp(spread * noise) if base else spread * noise
        out[name] = jnp.asarray(drawn.astype(out[name].dtype))
    for name, factor in factors.items():
        out[name] = (out[name] * factor).astype(out[name].dtype)
    return out
```

```python
import math
from contextlib import ExitStack, contextmanager

import numpy as np

import concourse.bass as bass
from concourse import mybir
from concourse.alu_op_type import AluOpType as ALU

ACT = mybir.ActivationFunctionType
F32 = mybir.dt.float32
BF16 = mybir.dt.bfloat16
I32 = mybir.dt.int32
I16 = mybir.dt.int16
U32 = mybir.dt.uint32
AX = mybir.AxisListType.X

P = 128
N, E, H, RBF, LAYERS, G = 3125, 100000, 48, 40, 4, 32
NB = -(-N // P)
NP = NB * P
LAST = N - (NB - 1) * P
TILES = -(-E // P)
TW = -(-TILES // 16) * 16
EP = TW * P
UNIT = 2 * P
RING = 8
UNITS = -(-(E // UNIT + NB) // RING) * RING
BODIES = UNITS // RING
LAG = 3
SLOTS = UNITS * UNIT
DUMP = SLOTS
REC = 44
R_CW, R_W1, R_DST, R_LOC = 40, 41, 42, 43
R2_W1, R2_SRC, R2_LOC = 0, 1, 2
BIG = float(2 ** 100)
NOMAX = float(2 ** 99)
C3, C9, T = 144, 432, 128
FC = 72
MC = 108
TAB0 = 84
TAB = 100
TAB1 = 52


class Link:

    def __init__(self, eng, sem):
        self.eng, self.sem, self.n = eng, sem, 0

    def __call__(self, ins):
        self.n += 1
        ins.then_inc(self.sem, 1)
        self.eng.wait_ge(self.sem, self.n)


@contextmanager
def stage(nc, name, *sems):
    handles = [nc.alloc_semaphore(f"{name}_{s}") for s in sems]
    with nc.Block(name) as block:
        yield (block, *handles)
    nc.clear_and_free_semaphores(handles)
    nc.all_engine_barrier()


class Memory:

    def __init__(self, nc, ctx):
        self.nc, self.ctx = nc, ctx

    def sb(self, name, shape, dt=F32):
        return self.ctx.enter_context(self.nc.sbuf_tensor(f"sb_{name}", shape, dt))


def bc(ap, n):
    return ap.unsqueeze(2).to_broadcast([ap.shape[0], ap.shape[1], n])


def along(ap, n):
    return ap.unsqueeze(1).to_broadcast([ap.shape[0], n, ap.shape[1]])



def constants(nc, m):
    c = {
        "iota": m.sb("iota_f32", [P, P]), "iota16": m.sb("iota_i16", [P, P], I16), "part": m.sb("iota_part", [P, 1]),
        "ident": m.sb("ident_f32", [P, P]), "identb": m.sb("ident_bf16", [P, P], BF16),
        "tri": m.sb("tri_bf16", [P, P], BF16), "ones": m.sb("ones_f32", [P, P]),
        "some": m.sb("ones_last", [P, P]), "onesb": m.sb("ones_bf16", [P, P], BF16),
    }
    with stage(nc, "const", "made", "written") as (block, made, written):
        @block.gpsimd
        def _(pool):
            pool.iota(c["iota"][:], [[1, P]], base=0, channel_multiplier=0, allow_small_or_imprecise_dtypes=True)
            pool.iota(c["iota16"][:], [[1, P]], base=0, channel_multiplier=0)
            pool.iota(c["part"][:], [[0, 1]], base=0, channel_multiplier=1,
                      allow_small_or_imprecise_dtypes=True).then_inc(made, 1)

        @block.vector
        def _(dve):
            dve.memset(c["ones"][:], 1.0)
            dve.memset(c["onesb"][:], 1.0)
            dve.wait_ge(made, 1)
            dve.tensor_scalar(c["some"][:], c["part"][:].to_broadcast([P, P]), float(LAST), None, ALU.is_lt)
            dve.tensor_scalar(c["ident"][:], c["iota"][:], c["part"][:, 0:1], None, ALU.is_equal)
            dve.tensor_scalar(c["identb"][:], c["iota"][:], c["part"][:, 0:1], None, ALU.is_equal)
            dve.tensor_scalar(c["tri"][:], c["iota"][:], c["part"][:, 0:1], None, ALU.is_gt)
    return c



def group(nc, c, ps, name, key_dram, big, pos, loc, blocks, starts):
    W3 = TW * NB
    onehot = big[:, 0:W3 // 2].bitcast(BF16).rearrange("p (t b) -> p t b", b=NB)
    within = big[:, W3 // 2:W3].bitcast(BF16).rearrange("p (t b) -> p t b", b=NB)
    before = big[:, W3:2 * W3 + NB].rearrange("p (t b) -> p t b", b=NB)
    with ExitStack() as ctx:
        m = Memory(nc, ctx)
        key = m.sb(f"{name}_key", [P, TW], I32)
        hi = m.sb(f"{name}_hi", [P, TW], I32)
        rank = m.sb(f"{name}_rank", [P, TW])
        one = m.sb(f"{name}_one", [P, TW])
        cnt = m.sb(f"{name}_cnt", [P, NB])
        cnti = m.sb(f"{name}_cnti", [P, NB], I32)
        cntu = m.sb(f"{name}_cntu", [P, NB], I32)
        units = m.sb(f"{name}_units", [P, NB])
        start = m.sb(f"{name}_start", [P, NB + 1])
        uid = m.sb(f"{name}_uid", [P, UNITS])
        blk = m.sb(f"{name}_blk", [P, LAG + UNITS + RING])
        step = m.sb(f"{name}_step", [P, UNITS + RING + LAG - 1])
        word = m.sb(f"{name}_word", [P, BODIES + 1])
        dump = m.sb(f"{name}_dump", [P, TW - TILES + 1])
        STEP = 16
        with stage(nc, name, "key", "made", "onehot", "counted", "copied_w", "copied_s", "done") as (
                block, s_key, s_made, s_onehot, s_counted, s_w, s_s, s_done):
            @block.sync
            def _(sp):
                sp.dma_start(key[:], key_dram).then_inc(s_key, 16)

            @block.gpsimd
            def _(pool):
                pool.iota(uid[:], [[1, UNITS]], base=0, channel_multiplier=0, allow_small_or_imprecise_dtypes=True)
                pool.iota(dump[:], [[P, TW - TILES + 1]], base=DUMP, channel_multiplier=1,
                          allow_small_or_imprecise_dtypes=True).then_inc(s_made, 1)

            @block.tensor
            def _(pe):
                pe.wait_ge(s_onehot, 1)
                for j in range(TW // STEP):
                    if j >= 4:
                        pe.wait_ge(s_w, j - 3)
                        pe.wait_ge(s_s, j - 3)
                    oh = onehot[:, STEP * j:STEP * j + STEP, :]
                    pe.matmul(ps[:, 2 * (j % 4), 0:STEP * NB], c["tri"][:], oh, start=True, stop=True)
                    pe.matmul(ps[:, 2 * (j % 4) + 1, 0:STEP * NB], c["onesb"][:], oh, start=True,
                              stop=True).then_inc(s_counted, 1)

            @block.scalar
            def _(act):
                for j in range(TW // STEP):
                    act.wait_ge(s_counted, j + 1)
                    act.copy(within[:, STEP * j:STEP * j + STEP, :],
                             ps[:, 2 * (j % 4), 0:STEP * NB].rearrange("p (t b) -> p t b", b=NB)).then_inc(s_w, 1)

            @block.vector
            def _(dve):
                link = Link(dve, s_done)
                dve.memset(one[:], 1.0)
                dve.memset(before[:, 0:1, :], 0.0)
                dve.wait_ge(s_key, 16)
                link(dve.tensor_scalar(hi[:], key[:], 7, None, ALU.arith_shift_right))
                dve.wait_ge(s_made, 1)
                dve.tensor_tensor(onehot, bc(hi[:], NB), along(uid[:, 0:NB], TW), ALU.is_equal).then_inc(s_onehot, 1)
                link(dve.tensor_scalar(key[:], key[:], 127, None, ALU.bitwise_and))
                link(dve.tensor_copy(loc, key[:]))
                for j in range(TW // STEP):
                    dve.wait_ge(s_counted, j + 1)
                    dve.tensor_copy(before[:, STEP * j + 1:STEP * j + STEP + 1, :],
                                    ps[:, 2 * (j % 4) + 1, 0:STEP * NB].rearrange("p (t b) -> p t b", b=NB)
                                    ).then_inc(s_s, 1)
                dve.wait_ge(s_s, TW // STEP)
                for b in range(NB):
                    ins = dve.tensor_tensor_scan(before[:, 1:TW + 1, b], one[:], before[:, 1:TW + 1, b], 0.0,
                                                 ALU.mult, ALU.add)
                link(ins)
                link(dve.tensor_scalar(cnt[:], before[:, TW, :], float(UNIT - 1), None, ALU.add))
                link(dve.tensor_copy(cnti[:], cnt[:]))
                link(dve.tensor_scalar(cntu[:], cnti[:], 8, None, ALU.arith_shift_right))
                link(dve.tensor_copy(units[:], cntu[:]))
                link(dve.tensor_scalar(units[:], units[:], 1.0, None, ALU.max))
                link(dve.memset(start[:, 0:1], 0.0))
                link(dve.tensor_tensor_scan(start[:, 1:NB + 1], one[:, 0:NB], units[:], 0.0, ALU.mult, ALU.add))
                link(dve.tensor_copy(starts, start[:]))
                link(dve.tensor_scalar(cnt[:], start[:, 0:NB], float(UNIT), None, ALU.mult))
                dve.wait_ge(s_w, TW // STEP)
                link(dve.tensor_tensor(before[:, 0:TW, :], before[:, 0:TW, :], within, ALU.add))
                link(dve.tensor_tensor(before[:, 0:TW, :], before[:, 0:TW, :], along(cnt[:], TW), ALU.add))
                link(dve.tensor_tensor(before[:, 0:TW, :], before[:, 0:TW, :], onehot, ALU.mult))
                link(dve.tensor_reduce(rank[:], before[:, 0:TW, :], AX, ALU.add))
                first = E - (TILES - 1) * P
                for a in range(first, P, 32):
                    link(dve.tensor_copy(rank[a:a + 32, TILES - 1:TILES], dump[a:a + 32, 0:1]))
                link(dve.tensor_copy(rank[:, TILES:TW], dump[:, 1:TW - TILES + 1]))
                link(dve.tensor_copy(pos, rank[:]))
                ge = big[:, 0:UNITS * NB].rearrange("p (u b) -> p u b", b=NB)
                link(dve.memset(blk[:, 0:LAG], 0.0))
                link(dve.tensor_tensor(ge, bc(uid[:], NB), along(start[:, 0:NB], UNITS), ALU.is_ge))
                link(dve.tensor_reduce(blk[:, LAG:LAG + UNITS], ge, AX, ALU.add))
                link(dve.tensor_scalar(blk[:, LAG:LAG + UNITS], blk[:, LAG:LAG + UNITS], -1.0, None, ALU.add))
                link(dve.memset(blk[:, LAG + UNITS:], float(NB - 1)))
                link(dve.tensor_tensor(step[:], blk[:, 1:], blk[:, 0:UNITS + RING + LAG - 1], ALU.subtract))
                first = blk[:, 0:UNITS + RING].rearrange("p (i k) -> p i k", k=RING)[:, :, 0]
                link(dve.tensor_scalar(word[:], first, 0.0, None, ALU.add))
                for k in range(RING + LAG - 1):
                    s = step[:, k:k + UNITS + 1:RING]
                    link(dve.scalar_tensor_tensor(word[:], s, float(32 << k), word[:], ALU.mult, ALU.add))
                link(dve.tensor_copy(blocks, word[:]))


def prefill(nc, m, lists, sem):
    n = 0
    for name, dram, width, place in lists:
        rows = SLOTS // P
        step = rows // 64
        pad = m.sb(f"{name}_pad", [P, step, width])
        with stage(nc, f"{name}_prefill", "made") as (block, made):
            @block.vector
            def _(dve):
                link = Link(dve, made)
                link(dve.memset(pad[:], 0.0))
                link(dve.memset(pad[:, :, place:place + 1], -1.0))

            @block.sync
            def _(sp):
                sp.wait_ge(made, 2)
                view = dram[0:SLOTS, :].rearrange("(p r) w -> p r w", p=P)
                for j in range(64):
                    sp.dma_start(view[:, step * j:step * j + step, :], pad[:]).then_inc(sem, 16)
        n += 16 * 64
    return n


def scatter(nc, name, meta, pos, rec_dram, width, feat_dram, filled, filled_n):
    HALF = 8
    nf = width - meta.shape[2]
    with ExitStack() as ctx:
        m = Memory(nc, ctx)
        rec = m.sb(f"{name}_rec", [P, 2, HALF, width])
        idx = m.sb(f"{name}_idx", [P, 2, HALF], U32)
        with stage(nc, name, "feat0", "feat1", "ready", "sent0", "sent1", "passed") as (
                block, f0, f1, ready, sent0, sent1, passed):
            feat, sent = (f0, f1), (sent0, sent1)

            if nf:
                @block.sync
                def _(sp):
                    def body(i):
                        for h in range(2):
                            if not isinstance(i, int):
                                sp.wait_ge(sent[h], i * (16 * HALF))
                            sp.dma_start(rec[:, h, :, 0:nf], feat_dram[:, bass.ds(i * (2 * HALF) + h * HALF, HALF), :]
                                         ).then_inc(feat[h], 16)
                    body(0)
                    with sp.Fori(1, TW // (2 * HALF)) as i:
                        body(i)

            @block.vector
            def _(dve):
                def body(i):
                    for h in range(2):
                        t = i * (2 * HALF) + h * HALF
                        if not isinstance(i, int):
                            dve.wait_ge(sent[h], i * (16 * HALF))
                        dve.tensor_copy(rec[:, h, :, nf:width], meta[:, bass.ds(t, HALF), :])
                        dve.tensor_copy(idx[:, h, :], pos[:, bass.ds(t, HALF)]).then_inc(ready, 1)
                body(0)
                with dve.Fori(1, TW // (2 * HALF)) as i:
                    body(i)

            @block.gpsimd
            def _(pool):
                pool.wait_ge(filled, filled_n)

                def body(i):
                    for h in range(2):
                        pool.wait_ge(ready, i * 2 + h + 1)
                        if nf:
                            pool.wait_ge(feat[h], i * 16 + 16)
                        pool.sem_inc(passed, 1)
                        for j in range(HALF):
                            pool.indirect_dma_start(rec_dram, bass.IndirectOffsetOnAxis(idx[:, h, j:j + 1], 0),
                                                    rec[:, h, j, :], None).then_inc(sent[h], 16)
                body(0)
                with pool.Fori(1, TW // (2 * HALF)) as i:
                    body(i)
                for h in range(2):
                    pool.wait_ge(sent[h], 16 * HALF * (TW // (2 * HALF)))



def layer_norm(nc, name, x, out, tmp, gain=None, bias=None, relu=False, add=None, eps=1e-5):
    f = x.shape[2]
    with ExitStack() as ctx:
        m = Memory(nc, ctx)
        mean = m.sb(f"{name}_mean", [P, NB])
        var = m.sb(f"{name}_var", [P, NB])
        std = m.sb(f"{name}_std", [P, NB])
        with stage(nc, name, "step", "var", "std") as (block, step, s_var, s_std):
            @block.vector
            def _(dve):
                link = Link(dve, step)
                link(dve.tensor_reduce(mean[:], x, AX, ALU.add))
                link(dve.tensor_scalar(mean[:], mean[:], 1.0 / f, None, ALU.mult))
                link(dve.tensor_tensor(out, x, bc(mean[:], f), ALU.subtract))
                link(dve.tensor_tensor(tmp, out, out, ALU.mult))
                link(dve.tensor_reduce(var[:], tmp, AX, ALU.add))
                dve.tensor_scalar(var[:], var[:], 1.0 / f, eps, ALU.mult, ALU.add).then_inc(s_var, 1)
                dve.wait_ge(s_std, 1)
                link(dve.reciprocal(std[:], std[:]))
                link(dve.tensor_tensor(out, out, bc(std[:], f), ALU.mult))
                if gain is not None:
                    link(dve.tensor_tensor(out, out, along(gain, NB), ALU.mult))
                    link(dve.tensor_tensor(out, out, along(bias, NB), ALU.add))
                if relu:
                    link(dve.tensor_scalar(out, out, 0.0, None, ALU.max))
                if add is not None:
                    link(dve.tensor_tensor(out, out, add, ALU.add))

            @block.scalar
            def _(act):
                act.wait_ge(s_var, 1)
                act.sqrt(std[:], var[:]).then_inc(s_std, 1)


def turn(nc, c, ps, name, x, xT):
    f = x.shape[2]
    with stage(nc, name, "turned", "copied") as (block, turned, copied):
        groups = [range(b, min(b + 4, NB)) for b in range(0, NB, 4)]

        @block.tensor
        def _(pe):
            for g, bs in enumerate(groups):
                for j, b in enumerate(bs):
                    ins = pe.transpose(ps[0:f, g, P * j:P * j + P], x[:, b, :], c["ident"][:])
                ins.then_inc(turned, 1)

        @block.scalar
        def _(act):
            for g, bs in enumerate(groups):
                act.wait_ge(turned, g + 1)
                n = len(bs) * P
                act.copy(xT[0:f, 4 * P * g:4 * P * g + n], ps[0:f, g, 0:n]).then_inc(copied, 1)


def times(nc, ps, name, xT, w, out):
    k, f = w.shape
    per = 5 if f <= 100 else 3
    groups = [range(b, min(b + per, NB)) for b in range(0, NB, per)]
    with stage(nc, name, "summed", "copied") as (block, summed, copied):
        @block.tensor
        def _(pe):
            for g, bs in enumerate(groups):
                if g >= 8:
                    pe.wait_ge(copied, g - 7)
                for j, b in enumerate(bs):
                    ins = pe.matmul(ps[:, g % 8, f * j:f * j + f], xT[0:k, P * b:P * b + P], w, start=True, stop=True)
                ins.then_inc(summed, 1)

        @block.scalar
        def _(act):
            for g, bs in enumerate(groups):
                act.wait_ge(summed, g + 1)
                act.copy(out[:, bs[0]:bs[-1] + 1, :],
                         ps[:, g % 8, 0:f * len(bs)].rearrange("p (b f) -> p b f", f=f)).then_inc(copied, 1)


def send(nc, name, pairs):
    with stage(nc, name, "landed") as (block, landed):
        @block.sync
        def _(sp):
            for dst, src in pairs:
                sp.dma_start(dst, src).then_inc(landed, 16)
            sp.wait_ge(landed, 16 * len(pairs))


def over_units(eng, pieces, blocks=None):
    deepest = max(lag for lag, _ in pieces)

    def body(i, begin, end):
        of = {}
        if blocks is not None:
            word = eng.value_load(blocks[0:1, bass.ds(i, 1)], min_val=0, max_val=2 ** (5 + RING + LAG) - 1)
            of[-LAG] = eng.snap(word & 31).with_bounds(min_val=0, max_val=NB - 1)
            for k in range(1 - LAG, 0 if end else RING):
                of[k] = eng.snap(of[k - 1] + ((word >> (4 + LAG + k)) & 1)).with_bounds(min_val=0, max_val=NB - 1)
        for k in range(deepest if end else RING):
            for lag, piece in pieces:
                if (begin and k < lag) or (end and k >= lag):
                    continue
                rnd = i if k >= lag else i - 1
                piece(i * RING + (k - lag), (k - lag) % RING, rnd, of.get(k - lag))

    body(0, True, False)
    with eng.Fori(1, BODIES) as i:
        body(i, False, False)
    if deepest:
        body(BODIES, False, True)


def reused(u, ring):
    return not isinstance(u, int) or u >= ring


def load_records(rec, rec_dram, arrived, freed):
    view = rec_dram[0:SLOTS, :].rearrange("(u j p) w -> u p j w", j=2, p=P)

    def program(sp):
        def piece(u, k, rnd, b):
            if reused(u, RING):
                for sem in freed:
                    sp.wait_ge(sem, u - RING + 1)
            src = view[bass.ds(u, 1)].rearrange("o p j w -> (o p) j w")
            sp.dma_start(rec[:, k, :, :], src).then_inc(arrived[k], 16)
        over_units(sp, [(0, piece)])
    return program


def gather_rows(rec, word, table, rows, arrived, gathered, used, passed):
    def program(pool):
        def piece(u, k, rnd, b):
            pool.wait_ge(arrived[k], rnd * 16 + 16)
            if reused(u, RING):
                pool.wait_ge(used, u - RING + 1)
            pool.sem_inc(passed, 1)
            for j in range(2):
                pool.indirect_dma_start(rows[:, k, j, :], None, table,
                                        bass.IndirectOffsetOnAxis(rec[:, k, j, word:word + 1].bitcast(U32), 0)
                                        ).then_inc(gathered[k], 16)
        over_units(pool, [(0, piece)])
    return program


def gate_edges(nc, c, ps, name, rec_dram, table, embn, w, blocks, acc):
    with ExitStack() as ctx:
        m = Memory(nc, ctx)
        rec = m.sb(f"{name}_rec", [P, RING, 2, REC])
        rows = m.sb(f"{name}_rows", [P, RING, 2, TAB0])
        hot = m.sb(f"{name}_hot", [P, 4, 2, P])
        attrT = m.sb(f"{name}_attrT", [RBF, 2, UNIT])
        hotT = m.sb(f"{name}_hotT", [P, 2, UNIT])
        hid = m.sb(f"{name}_hid", [64, 2, UNIT])
        prod = m.sb(f"{name}_prod", [P, 2, G])
        dots = m.sb(f"{name}_dots", [P, 2])
        wgt = m.sb(f"{name}_wgt", [P, 2])
        msg = m.sb(f"{name}_msg", [P, 2, 2, H + 1])
        names = ["ones", "hot", "turned", "copied", "mixed", "silu", "gated", "msg", "summed", "added", "link", "passed"]
        with stage(nc, name, *names, *[f"rec{k}" for k in range(RING)], *[f"row{k}" for k in range(RING)]) as (
                block, s_ones, s_hot, s_turned, s_copied, s_mixed, s_silu, s_gated, s_msg, s_summed, s_added, s_link, s_passed,
                *dmas):
            arrived, gathered = dmas[:RING], dmas[RING:]
            block.sync(load_records(rec, rec_dram, arrived, [s_msg, s_turned]))
            block.gpsimd(gather_rows(rec, R_DST, table, rows, arrived, gathered, s_msg, s_passed))

            @block.tensor
            def _(pe):
                def turn_in(u, k, rnd, b):
                    pe.wait_ge(arrived[k], rnd * 16 + 16)
                    pe.wait_ge(s_hot, u + 1)
                    if reused(u, 1):
                        pe.wait_ge(s_copied, u * 2)
                    for j in range(2):
                        pe.transpose(ps[:, 1, P * j:P * j + P], hot[:, k % 4, j, :], c["ident"][:])
                    for j in range(2):
                        ins = pe.transpose(ps[0:RBF, 0, P * j:P * j + P], rec[:, k, j, 0:RBF], c["ident"][:])
                    ins.then_inc(s_turned, 1)

                def mix(u, k, rnd, b):
                    pe.wait_ge(s_copied, u * 2 + 2)
                    if reused(u, 2):
                        pe.wait_ge(s_silu, u - 1)
                        pe.wait_ge(s_msg, u - 1)
                    for j in range(2):
                        pe.matmul(ps[:, 4 + k % 2, 128 + G * j:128 + G * j + G], hotT[:, k % 2, P * j:P * j + P],
                                  embn[:, bass.ds(b, 1), :].rearrange("p o f -> p (o f)"), start=True, stop=True)
                    pe.matmul(ps[0:H, 2 + k % 2, 0:UNIT], w["F1W"][:], attrT[:, k % 2, :], start=True, stop=True
                              ).then_inc(s_mixed, 1)

                def gate(u, k, rnd, b):
                    pe.wait_ge(s_silu, u + 1)
                    for j in range(2):
                        ins = pe.matmul(ps[:, 4 + k % 2, H * j:H * j + H], hid[0:H + 1, k % 2, P * j:P * j + P],
                                        w["F2"][:], start=True, stop=True)
                    ins.then_inc(s_gated, 1)

                def total(u, k, rnd, b):
                    pe.wait_ge(s_msg, u + 1)
                    if reused(u, 2):
                        pe.wait_ge(s_added, u - 1)
                    for j in range(2):
                        ins = pe.matmul(ps[:, 6 + k % 2, 0:H + 1], hot[:, k % 4, j, :], msg[:, k % 2, j, :],
                                        start=(j == 0), stop=(j == 1))
                    ins.then_inc(s_summed, 1)
                over_units(pe, [(0, turn_in), (1, mix), (2, gate), (3, total)], blocks)

            @block.scalar
            def _(act):
                def copy_in(u, k, rnd, b):
                    act.wait_ge(s_turned, u + 1)
                    if reused(u, 2):
                        act.wait_ge(s_mixed, u - 1)
                    act.copy(attrT[:, k % 2, :], ps[0:RBF, 0, 0:UNIT]).then_inc(s_copied, 1)
                    act.copy(hotT[:, k % 2, :], ps[:, 1, 0:UNIT]).then_inc(s_copied, 1)

                def silu(u, k, rnd, b):
                    act.wait_ge(s_mixed, u + 1)
                    if reused(u, 1):
                        act.wait_ge(s_ones, 1)
                    if reused(u, 2):
                        act.wait_ge(s_gated, u - 1)
                    act.activation(hid[0:H, k % 2, :], ps[0:H, 2 + k % 2, 0:UNIT], ACT.Silu, bias=w["F1b"][:]
                                   ).then_inc(s_silu, 1)
                act.wait_ge(s_ones, 1)
                over_units(act, [(0, copy_in), (1, silu)])

            @block.vector
            def _(dve):
                dve.memset(hid[:], 1.0).then_inc(s_ones, 1)

                def one_hot(u, k, rnd, b):
                    dve.wait_ge(arrived[k], rnd * 16 + 16)
                    if reused(u, 4):
                        dve.wait_ge(s_summed, u - 3)
                    for j in range(2):
                        ins = dve.tensor_scalar(hot[:, k % 4, j, :], c["iota"][:], rec[:, k, j, R_LOC:R_LOC + 1], None,
                                                ALU.is_equal)
                    ins.then_inc(s_hot, 1)

                def message(u, k, rnd, b):
                    dve.wait_ge(gathered[k], rnd * 32 + 32)
                    dve.wait_ge(s_gated, u + 1)
                    if reused(u, 2):
                        dve.wait_ge(s_summed, u - 1)
                    if reused(u, 1):
                        dve.wait_ge(s_msg, u)
                    base = u * 4
                    x = rows[:, k]
                    o = msg[:, k % 2]
                    dve.tensor_tensor(prod[:], ps[:, 4 + k % 2, 128:128 + 2 * G].rearrange("p (j f) -> p j f", f=G),
                                      x[:, :, H:H + G], ALU.mult).then_inc(s_link, 1)
                    dve.tensor_tensor(wgt[:], rec[:, k, :, R_CW], x[:, :, H + G], ALU.mult).then_inc(s_link, 1)
                    dve.wait_ge(s_link, base + 2)
                    dve.tensor_reduce(dots[:], prod[:], AX, ALU.add).then_inc(s_link, 1)
                    dve.tensor_copy(o[:, :, H:H + 1], x[:, :, H + G:H + G + 1])
                    dve.wait_ge(s_link, base + 3)
                    for j in range(2):
                        ins = dve.scalar_tensor_tensor(o[:, j, 0:H], ps[:, 4 + k % 2, H * j:H * j + H],
                                                       dots[:, j:j + 1], x[:, j, 0:H], ALU.add, ALU.mult)
                    ins.then_inc(s_link, 1)
                    dve.wait_ge(s_link, base + 4)
                    dve.tensor_tensor(o[:, :, 0:H], o[:, :, 0:H], bc(wgt[:], H), ALU.mult).then_inc(s_msg, 1)

                def add(u, k, rnd, b):
                    dve.wait_ge(s_summed, u + 1)
                    if reused(u, 1):
                        dve.wait_ge(s_added, u)
                    a = acc[:, bass.ds(b, 1), :].rearrange("p o f -> p (o f)")
                    dve.tensor_tensor(a, a, ps[:, 6 + k % 2, 0:H + 1], ALU.add).then_inc(s_added, 1)
                over_units(dve, [(0, one_hot), (2, message), (3, add)], blocks)


def attend(nc, c, ps, name, rec_dram, width, place, other, score, table, tab, at_h, queryT, blocks, acc, nmax):
    with ExitStack() as ctx:
        m = Memory(nc, ctx)
        rec = m.sb(f"{name}_rec", [P, RING, 2, width])
        rows = m.sb(f"{name}_rows", [P, RING, 2, tab])
        out_of = m.sb(f"{name}_out_of", [P, 2, 2, P], F32 if score is not None else BF16)
        prob = m.sb(f"{name}_prob", [P, 2, UNIT])
        probT = m.sb(f"{name}_probT", [P, 2, UNIT])
        top = m.sb(f"{name}_top", [P, RING])
        ntop = m.sb(f"{name}_ntop", [P, RING])
        fall = m.sb(f"{name}_fall", [P, RING])
        shrink = m.sb(f"{name}_shrink", [P, RING])
        keyT = m.sb(f"{name}_keyT", [H + 1, 2, UNIT])
        query = m.sb(f"{name}_query", [H + 1, 2, P])
        names = ["key", "outof", "turned", "copied", "query", "scored", "maxed", "prob", "shrunk", "turnedp", "copiedp",
                 "summed", "added", "biased", "linka", "linkb", "passed", "passedpe"]
        with stage(nc, name, *names, *[f"rec{k}" for k in range(RING)], *[f"row{k}" for k in range(RING)]) as (
                block, s_key, s_outof, s_turned, s_copied, s_query, s_scored, s_maxed, s_prob, s_shrunk, s_turnedp,
                s_copiedp, s_summed, s_added, s_biased, s_linka, s_linkb, s_passed, s_passed_pe, *dmas):
            arrived, gathered = dmas[:RING], dmas[RING:]
            block.sync(load_records(rec, rec_dram, arrived, [s_biased, s_summed] if score is not None else [s_key, s_outof]))
            block.gpsimd(gather_rows(rec, other, table, rows, arrived, gathered, s_summed, s_passed))

            @block.tensor
            def _(pe):
                def turn_keys(u, k, rnd, b):
                    pe.wait_ge(s_key, u + 1)
                    if reused(u, 2):
                        pe.wait_ge(s_copied, u - 1)
                    pe.sem_inc(s_passed_pe, 1)
                    for j in range(2):
                        ins = pe.transpose(ps[0:H + 1, k % 2, P * j:P * j + P], rows[:, k, j, 0:H + 1], c["ident"][:])
                    ins.then_inc(s_turned, 1)

                def scores(u, k, rnd, b):
                    if reused(u, 2):
                        pe.wait_ge(s_prob, u - 1)
                    bank = ps[:, 2 + k % 2, :]
                    if score is not None:
                        pe.wait_ge(s_biased, u + 1)
                        for j in range(2):
                            ins = pe.transpose(bank[:, P * j:P * j + P], out_of[:, k % 2, j, :], c["ident"][:])
                    else:
                        pe.wait_ge(s_copied, u + 1)
                        pe.wait_ge(s_query, u + 1)
                        pe.wait_ge(s_outof, u + 1)
                        pe.matmul(bank[:, 0:UNIT], query[:, k % 2, :], keyT[:, k % 2, :], start=True, stop=False)
                        for j in range(2):
                            ins = pe.matmul(bank[:, P * j:P * j + P], out_of[:, k % 2, j, :], c["identb"][:],
                                            start=False, stop=(j == 1))
                    ins.then_inc(s_scored, 1)

                def turn_probs(u, k, rnd, b):
                    pe.wait_ge(s_prob, u + 1)
                    if reused(u, 2):
                        pe.wait_ge(s_copiedp, u - 1)
                    for j in range(2):
                        ins = pe.transpose(ps[:, 4 + k % 2, P * j:P * j + P], prob[:, k % 2, P * j:P * j + P],
                                           c["ident"][:])
                    ins.then_inc(s_turnedp, 1)

                def sums(u, k, rnd, b):
                    pe.wait_ge(s_copiedp, u + 1)
                    if score is not None:
                        pe.wait_ge(gathered[k], rnd * 32 + 32)
                    if reused(u, 2):
                        pe.wait_ge(s_added, u - 1)
                    for j in range(2):
                        ins = pe.matmul(ps[:, 6 + k % 2, 0:H + 1], probT[:, k % 2, P * j:P * j + P],
                                        rows[:, k, j, at_h:at_h + H + 1], start=(j == 0), stop=(j == 1))
                    ins.then_inc(s_summed, 1)
                pieces = [(1, scores), (2, turn_probs), (3, sums)]
                over_units(pe, ([(0, turn_keys)] if score is None else []) + pieces)

            @block.scalar
            def _(act):
                def exps(u, k, rnd, b):
                    act.wait_ge(s_maxed, u + 1)
                    if reused(u, 2):
                        act.wait_ge(s_turnedp, u - 1)
                    act.activation(prob[:, k % 2, :], ps[:, 2 + k % 2, 0:UNIT], ACT.Exp, bias=ntop[:, k:k + 1]
                                   ).then_inc(s_prob, 1)
                    act.activation(shrink[:, k:k + 1], fall[:, k:k + 1], ACT.Exp).then_inc(s_shrunk, 1)

                def copy_keys(u, k, rnd, b):
                    act.wait_ge(s_turned, u + 1)
                    if reused(u, 2):
                        act.wait_ge(s_scored, u - 1)
                    act.copy(query[:, k % 2, :], queryT[0:H + 1, bass.ds(b * P, P)]).then_inc(s_query, 1)
                    act.copy(keyT[:, k % 2, :], ps[0:H + 1, k % 2, 0:UNIT]).then_inc(s_copied, 1)

                def bias(u, k, rnd, b):
                    act.wait_ge(s_outof, u + 1)
                    for j in range(2):
                        ins = act.activation(out_of[:, k % 2, j, :], out_of[:, k % 2, j, :], ACT.Identity,
                                             bias=rec[:, k, j, score:score + 1])
                    ins.then_inc(s_biased, 1)
                if score is None:
                    over_units(act, [(0, copy_keys), (1, exps)], blocks)
                else:
                    over_units(act, [(0, bias), (1, exps)])

            @block.vector
            def _(dve):
                def place_out(u, k, rnd, b):
                    dve.wait_ge(arrived[k], rnd * 16 + 16)
                    if reused(u, 2):
                        dve.wait_ge(s_scored, u - 1)
                    if score is None:
                        dve.wait_ge(gathered[k], rnd * 32 + 32)
                        dve.scalar_tensor_tensor(rows[:, k, :, 0:RBF], rec[:, k, :, 0:RBF], 0.1, rows[:, k, :, 0:RBF],
                                                 ALU.mult, ALU.add).then_inc(s_key, 1)
                    for j in range(2):
                        ins = dve.tensor_scalar(out_of[:, k % 2, j, :], c["iota"][:] if score is not None
                                                else c["iota16"][:], rec[:, k, j, place:place + 1], -BIG,
                                                ALU.not_equal, ALU.mult)
                    ins.then_inc(s_outof, 1)

                def maxima(u, k, rnd, b):
                    dve.wait_ge(s_scored, u + 1)
                    dve.tensor_reduce(top[:, k:k + 1], ps[:, 2 + k % 2, 0:UNIT], AX, ALU.max).then_inc(s_linka, 1)
                    nm = nmax[:, bass.ds(b, 1)]
                    dve.wait_ge(s_linka, u + 1)
                    if reused(u, 1):
                        dve.wait_ge(s_maxed, u)
                    dve.tensor_scalar(ntop[:, k:k + 1], top[:, k:k + 1], -1.0, nm, ALU.mult, ALU.min
                                      ).then_inc(s_linkb, 1)
                    dve.wait_ge(s_linkb, u * 2 + 1)
                    dve.tensor_tensor(fall[:, k:k + 1], ntop[:, k:k + 1], nm, ALU.subtract).then_inc(s_linkb, 1)
                    dve.wait_ge(s_linkb, u * 2 + 2)
                    dve.tensor_scalar(nm, ntop[:, k:k + 1], 0.0, None, ALU.add).then_inc(s_maxed, 1)

                def copy_probs(u, k, rnd, b):
                    dve.wait_ge(s_turnedp, u + 1)
                    if reused(u, 2):
                        dve.wait_ge(s_summed, u - 1)
                    dve.tensor_copy(probT[:, k % 2, :], ps[:, 4 + k % 2, 0:UNIT]).then_inc(s_copiedp, 1)

                def add(u, k, rnd, b):
                    dve.wait_ge(s_summed, u + 1)
                    dve.wait_ge(s_shrunk, u + 1)
                    if reused(u, 1):
                        dve.wait_ge(s_added, u)
                    a = acc[:, bass.ds(b, 1), :].rearrange("p o f -> p (o f)")
                    dve.scalar_tensor_tensor(a, a, shrink[:, k:k + 1], ps[:, 6 + k % 2, 0:H + 1], ALU.mult, ALU.add
                                             ).then_inc(s_added, 1)
                over_units(dve, [(0, place_out), (1, maxima), (2, copy_probs), (3, add)], blocks)


def first_part(nc, c, m, ps, a, x, h, tmp, rec_dram, blocks, upto=None):
    S = m
    table0 = nc.dram_tensor("table0", [NP, TAB0], F32).ap()
    table = nc.dram_tensor("table", [NP, TAB], F32).ap()
    rows_of = lambda t: t.rearrange("(b p) w -> p b w", p=P)
    mult, logm = S.sb("mult", [P, NB]), S.sb("logm", [P, NB])
    acc = S.sb("acc", [P, NB, H + 1])
    nmax = S.sb("nmax", [P, NB])
    tab = S.sb("tab", [P, NB, TAB])
    xT = S.sb("xT", [P, NP])
    vec = S.sb("vec", [P, 8, H])
    w = {"F1W": S.sb("F1W", [RBF, H]), "F1b": S.sb("F1b", [H, 1]), "F2": S.sb("F2", [H + 1, H]),
         "adapt": S.sb("adapt", [G, G])}
    everyone = lambda v: v.partition_broadcast(P)

    layer_norm(nc, "ln_in", x[:], h[:], tmp[:], relu=True)
    with ExitStack() as ctx:
        t = Memory(nc, ctx)
        z = t.sb("z", [P, NB], U32)
        embn = t.sb("embn", [P, NB, G])
        tab0 = t.sb("tab0", [P, NB, TAB0])
        send(nc, "load0", [(z[:].bitcast(I32), a["node_type"]),
                           (mult[:], a["node_vec"]),
                           (w["F1W"][:], a["F1W"]), (w["F1b"][:], a["F1b"].rearrange("(f o) -> f o", o=1)),
                           (w["F2"][0:H, :], a["F2W"]), (w["F2"][H:H + 1, :], a["F2b"].rearrange("(o f) -> o f", o=1)),
                           (w["adapt"][:], a["adapt"])])
        with stage(nc, "emb", "gathered", "step") as (block, gathered, step):
            @block.gpsimd
            def _(pool):
                for b in range(NB):
                    pool.indirect_dma_start(embn[:, b, :], None, a["emb"],
                                            bass.IndirectOffsetOnAxis(z[:, b:b + 1], 0)).then_inc(gathered, 16)
                pool.wait_ge(gathered, 16 * NB)

            @block.vector
            def _(dve):
                link = Link(dve, step)
                dve.memset(tab0[:, :, H + G:TAB0], 0.0)
                dve.memset(acc[:], 0.0)
                link(dve.tensor_copy(tab0[:, :, 0:H], h[:]))
                link(dve.tensor_copy(tab0[:, :, H + G], mult[:]))
                link(dve.tensor_scalar(logm[:], mult[:], 1.0, None, ALU.max))

            @block.scalar
            def _(act):
                act.wait_ge(step, 3)
                act.activation(logm[:], logm[:], ACT.Ln)
        turn(nc, c, ps, "embT", embn[:], xT)
        times(nc, ps, "adapted", xT, w["adapt"][:], tab0[:, :, H:H + G])
        send(nc, "table0_out", [(rows_of(table0), tab0[:])])
        gate_edges(nc, c, ps, "gate", rec_dram, table0, embn, w, blocks, acc)
    if upto == "gate":
        return acc
    recip = S.sb("recip", [P, NB])

    def divide(name, floor):
        with stage(nc, name, "step") as (block, step):
            @block.vector
            def _(dve):
                link = Link(dve, step)
                link(dve.tensor_scalar(recip[:], acc[:, :, H], floor, None, ALU.max))
                link(dve.reciprocal(recip[:], recip[:]))
                link(dve.tensor_tensor(acc[:, :, 0:H], acc[:, :, 0:H], bc(recip[:], H), ALU.mult))

    def clear(name):
        with stage(nc, name, "step") as (block, step):
            @block.vector
            def _(dve):
                dve.memset(acc[:], 0.0)
                dve.memset(nmax[:], NOMAX)

    def plus(name, out, p, q):
        with stage(nc, name, "step") as (block, step):
            @block.vector
            def _(dve):
                dve.tensor_tensor(out, p, q, ALU.add)

    send(nc, "load1", [(vec[:, 0, :], everyone(a["gn"])), (vec[:, 1, :], everyone(a["bn"]))])
    divide("mean0", 1e-8)
    plus("res0", h[:], h[:], acc[:, :, 0:H])
    layer_norm(nc, "ln0", h[:], h[:], tmp[:], gain=vec[:, 0, :], bias=vec[:, 1, :])

    wqk = S.sb("wqk", [H, 2 * H])
    wm, wmT, wub = S.sb("wm", [H, H]), S.sb("wmT", [H, H]), S.sb("wub", [H, H])
    wu = S.sb("wu", [64 + H, H])
    both = S.sb("both", [P, NB, 64 + H])[:]
    qk, q1 = both[:, :, 0:2 * H], S.sb("q1", [P, NB, H + 1])[:]
    queryT = S.sb("queryT", [H + 1, NP])
    with stage(nc, "wu_gap", "step") as (block, step):
        @block.vector
        def _(dve):
            dve.memset(wu[:], 0.0)
    with nc.Fori(0, LAYERS) as layer:
        at = lambda v: v[bass.ds(layer, 1)].rearrange("o k f -> (o k) f")
        row = lambda v: v[bass.ds(layer, 1), :].rearrange("o f -> (o f)").partition_broadcast(P)
        send(nc, "load_layer", [(wqk[:, 0:H], at(a["Wq"])), (wqk[:, H:2 * H], at(a["Wk"])), (wm[:], at(a["Wm"])),
                                (wu[0:H, :], a["Wu"][bass.ds(layer, 1), 0:H, :].rearrange("o k f -> (o k) f")),
                                (wub[:], a["Wu"][bass.ds(layer, 1), H:2 * H, :].rearrange("o k f -> (o k) f"))]
             + [(vec[:, n, :], row(a[v])) for n, v in enumerate(["gq", "bq", "gk", "bk", "go", "bo"])])
        with stage(nc, "weights", "turned", "copied", "summed") as (block, turned, copied, summed):
            @block.tensor
            def _(pe):
                pe.transpose(ps[0:H, 0, 0:H], wm[:], c["ident"][0:H, 0:H]).then_inc(turned, 1)
                pe.wait_ge(copied, 1)
                pe.matmul(ps[64:64 + H, 1, 0:H], wmT[:], wub[:], start=True, stop=True).then_inc(summed, 1)

            @block.vector
            def _(dve):
                dve.wait_ge(turned, 1)
                dve.tensor_copy(wmT[:], ps[0:H, 0, 0:H]).then_inc(copied, 1)
                dve.wait_ge(summed, 1)
                dve.tensor_copy(wu[64:64 + H, :], ps[64:64 + H, 1, 0:H])
        turn(nc, c, ps, "hT", h[:], xT)
        times(nc, ps, "qk", xT, wqk[:], qk)
        layer_norm(nc, "lnq", qk[:, :, 0:H], q1[:, :, 0:H], tmp[:], gain=vec[:, 0, :], bias=vec[:, 1, :])
        layer_norm(nc, "lnk", qk[:, :, H:2 * H], tab[:, :, 0:H], tmp[:], gain=vec[:, 2, :], bias=vec[:, 3, :])
        with stage(nc, "rows", "step") as (block, step):
            @block.vector
            def _(dve):
                dve.memset(q1[:, :, H:H + 1], 1.0)
                dve.tensor_copy(tab[:, :, H], logm[:])
                dve.tensor_copy(tab[:, :, H + 1:2 * H + 1], h[:])
                dve.memset(tab[:, :, 2 * H + 1:TAB], 1.0)
        turn(nc, c, ps, "qT", q1, queryT)
        send(nc, "table_out", [(rows_of(table), tab[:])])
        clear("clear")
        attend(nc, c, ps, "attend", rec_dram, REC, R_LOC, R_DST, None, table, TAB, H + 1, queryT, blocks, acc, nmax)
        if upto == "attend":
            return acc
        divide("mean", 1e-10)
        with stage(nc, "join", "step") as (block, step):
            @block.vector
            def _(dve):
                dve.memset(both[:, :, H:64], 0.0)
                dve.tensor_copy(both[:, :, 0:H], h[:])
                dve.tensor_copy(both[:, :, 64:64 + H], acc[:, :, 0:H])
        turn(nc, c, ps, "bothT", both, xT)
        times(nc, ps, "update", xT, wu[:], tmp[:])
        with stage(nc, "leaky", "step") as (block, step):
            @block.vector
            def _(dve):
                link = Link(dve, step)
                link(dve.scalar_tensor_tensor(tmp[:], tmp[:], 0.01, tmp[:], ALU.mult, ALU.max))
                link(dve.tensor_tensor(h[:], h[:], tmp[:], ALU.add))
        layer_norm(nc, "lnh", h[:], h[:], tmp[:], gain=vec[:, 4, :], bias=vec[:, 5, :])
    plus("res1", x[:], x[:], h[:])



def second_part(nc, c, m, ps, x, h, tmp, rec_dram, blocks):
    table = nc.dram_tensor("table1", [NP, TAB1], F32).ap()
    acc, nmax = m.sb("acc1", [P, NB, H + 1]), m.sb("nmax1", [P, NB])
    tab = m.sb("tab1", [P, NB, TAB1])
    recip = m.sb("recip1", [P, NB])
    layer_norm(nc, "ln1", x[:], h[:], tmp[:], relu=True)
    with stage(nc, "rows1", "step") as (block, step):
        @block.vector
        def _(dve):
            dve.tensor_copy(tab[:, :, 0:H], h[:])
            dve.memset(tab[:, :, H:TAB1], 1.0)
            dve.memset(acc[:], 0.0)
            dve.memset(nmax[:], NOMAX)
    send(nc, "table1_out", [(table.rearrange("(b p) w -> p b w", p=P), tab[:])])
    attend(nc, c, ps, "attend1", rec_dram, 4, R2_LOC, R2_SRC, R2_W1, table, TAB1, 0, None, blocks, acc, nmax)
    with stage(nc, "elu", "step", "exp") as (block, step, s_exp):
        @block.vector
        def _(dve):
            link = Link(dve, step)
            link(dve.tensor_scalar(recip[:], acc[:, :, H], 1e-30, None, ALU.max))
            link(dve.reciprocal(recip[:], recip[:]))
            link(dve.tensor_tensor(h[:], acc[:, :, 0:H], bc(recip[:], H), ALU.mult))
            link(dve.tensor_scalar(tmp[:], h[:], 0.0, None, ALU.min))
            dve.wait_ge(s_exp, 1)
            link(dve.scalar_tensor_tensor(h[:], h[:], 0.0, tmp[:], ALU.max, ALU.add))
            link(dve.scalar_tensor_tensor(x[:], h[:], -1.0, x[:], ALU.add, ALU.add))

        @block.scalar
        def _(act):
            act.wait_ge(step, 4)
            act.activation(tmp[:], tmp[:], ACT.Exp).then_inc(s_exp, 1)



def count_edges(nc, m, ps, rec_dram, starts, C):
    BANKS = [(k * 512, min(512, NP - k * 512)) for k in range(-(-NP // 512))]
    ACT_BANKS = 4
    meta = m.sb("cnt_meta", [P, 2 * UNITS, 2])
    ends = m.sb("cnt_ends", [P, 2 * UNITS])
    iota = m.sb("cnt_iota", [P, NP], I16)
    zero = m.sb("cnt_zero", [P, 512], BF16)
    wide = m.sb("cnt_wide", [P, 2, NP], BF16)
    hot = m.sb("cnt_hot", [P, 2, P], BF16)
    PIECES = 8
    with stage(nc, "count", "meta", "iota", "zero", "step", "made0", "made1", "used0", "used1", "full", "copied_a",
               "copied_v") as (block, s_meta, s_iota, s_zero, s_step, made0, made1, used0, used1, s_full, s_copied_a,
                               s_copied_v):
        made, used = (made0, made1), (used0, used1)

        def block_bounds(eng, b):
            read = lambda at: eng.value_load(starts[0:1, bass.ds(at, 1)], min_val=0, max_val=UNITS)
            return read(b), read(b + 1)

        @block.sync
        def _(sp):
            view = rec_dram[0:SLOTS, :].rearrange("(t p) w -> p t w", p=P)
            n = 2 * UNITS // PIECES
            for j in range(PIECES):
                sp.dma_start(meta[:, n * j:n * j + n, :], view[:, n * j:n * j + n, R_DST:R_LOC + 1]).then_inc(s_meta, 16)

        @block.gpsimd
        def _(pool):
            pool.iota(iota[:], [[1, NP]], base=0, channel_multiplier=0).then_inc(s_iota, 1)

        @block.vector
        def _(dve):
            dve.memset(zero[:], 0.0).then_inc(s_zero, 1)
            dve.sem_inc(s_copied_v, 1)
            dve.wait_ge(s_meta, 16 * PIECES)
            dve.tensor_copy(ends[:], meta[:, :, 0].bitcast(I32)).then_inc(s_step, 1)
            dve.wait_ge(s_step, 1)
            dve.wait_ge(s_iota, 1)
            with dve.Fori(0, NB) as b:
                first, end = block_bounds(dve, b)
                with dve.Fori(first, end) as u:
                    for j in range(2):
                        t = u * 2 + j
                        dve.wait_ge(used[j], u + 1)
                        dve.tensor_scalar(hot[:, j, :], iota[:, 0:P], meta[:, bass.ds(t, 1), 1], None, ALU.is_equal)
                        dve.tensor_scalar(wide[:, j, :], iota[:], ends[:, bass.ds(t, 1)], None, ALU.is_equal
                                          ).then_inc(made[j], 1)
                dve.wait_ge(s_full, b + 1)
                for n, (at, w) in enumerate(BANKS[ACT_BANKS:]):
                    ins = dve.tensor_copy(C[:, bass.ds(b, 1), at:at + w].rearrange("p o d -> p (o d)"),
                                          ps[:, ACT_BANKS + n, 0:w])
                ins.then_inc(s_copied_v, 1)

        @block.tensor
        def _(pe):
            for j in range(2):
                pe.sem_inc(used[j], 1)
            pe.wait_ge(s_zero, 1)
            with pe.Fori(0, NB) as b:
                first, end = block_bounds(pe, b)
                pe.wait_ge(s_copied_a, b + 1)
                pe.wait_ge(s_copied_v, b + 1)
                for n, (at, w) in enumerate(BANKS):
                    pe.matmul(ps[:, n, 0:w], zero[:, 0:P], zero[:, 0:w], start=True, stop=False)
                with pe.Fori(first, end) as u:
                    for j in range(2):
                        pe.wait_ge(made[j], u + 1)
                        for n, (at, w) in enumerate(BANKS):
                            ins = pe.matmul(ps[:, n, 0:w], hot[:, j, :], wide[:, j, at:at + w], start=False, stop=False)
                        ins.then_inc(used[j], 1)
                for n, (at, w) in enumerate(BANKS):
                    ins = pe.matmul(ps[:, n, 0:w], zero[:, 0:P], zero[:, 0:w], start=False, stop=True)
                ins.then_inc(s_full, 1)

        @block.scalar
        def _(act):
            act.sem_inc(s_copied_a, 1)
            with act.Fori(0, NB) as b:
                act.wait_ge(s_full, b + 1)
                for n, (at, w) in enumerate(BANKS[:ACT_BANKS]):
                    ins = act.copy(C[:, bass.ds(b, 1), at:at + w].rearrange("p o d -> p (o d)"), ps[:, n, 0:w])
                ins.then_inc(s_copied_a, 1)


def degrees(nc, c, m, ps, C, dinv, many):
    top, tops = m.sb("deg_top", [P, 1]), m.sb("deg_tops", [P, 2])
    with stage(nc, "degrees", "summed", "top", "turned", "step", "root") as (
            block, s_summed, s_top, s_turned, step, s_root):
        @block.tensor
        def _(pe):
            for d in range(NB):
                for s in range(NB):
                    ins = pe.matmul(ps[:, 0, d:d + 1], C[:, s, P * d:P * d + P], c["onesb"][:, 0:1],
                                    start=(s == 0), stop=(s == NB - 1))
            ins.then_inc(s_summed, 1)
            pe.wait_ge(s_top, 1)
            pe.transpose(ps[0:1, 1, 0:P], top[:], c["ident"][:]).then_inc(s_turned, 1)

        @block.vector
        def _(dve):
            link = Link(dve, step)
            half = NB // 2
            dve.tensor_reduce(tops[:, 0:1], C[:, 0:half].rearrange("p b d -> p (b d)"), AX, ALU.max)
            link(dve.tensor_reduce(tops[:, 1:2], C[:, half:].rearrange("p b d -> p (b d)"), AX, ALU.max))
            dve.tensor_tensor(top[:], tops[:, 0:1], tops[:, 1:2], ALU.max).then_inc(s_top, 1)
            dve.wait_ge(s_summed, 1)
            link(dve.tensor_scalar(dinv[:], ps[:, 0, 0:NB], 1.0, None, ALU.add))
            dve.wait_ge(s_turned, 1)
            link(dve.tensor_reduce(top[0:1, :], ps[0:1, 1, 0:P], AX, ALU.max))
            link(dve.tensor_scalar(top[0:1, :], top[0:1, :], 256.0, None, ALU.is_ge))
            link(dve.tensor_copy(many[0:1, :], top[0:1, :]))
            dve.wait_ge(s_root, 1)
            link(dve.reciprocal(dinv[:], dinv[:]))

        @block.scalar
        def _(act):
            act.wait_ge(step, 2)
            act.sqrt(dinv[:], dinv[:]).then_inc(s_root, 1)


class Spread:

    def __init__(self, nc, c, ps, C, dinv, many, rec_dram, blocks):
        self.nc, self.c, self.ps, self.C, self.dinv, self.many = nc, c, ps, C, dinv, many
        self.rec_dram, self.blocks = rec_dram, blocks
        self.table = nc.dram_tensor("table2", [NP, H], F32).ap()

    def __call__(self, name, g, out):
        with ExitStack() as ctx:
            m = Memory(self.nc, ctx)
            self.parts = m.sb(f"{name}_parts", [P, NB, 3, H], BF16)
            self.scaled = m.sb(f"{name}_scaled", [P, NB, H])
            self.run(name, g, out)

    def run(self, name, g, out):
        nc, ps, C, parts, scaled, dinv = self.nc, self.ps, self.C, self.parts, self.scaled, self.dinv
        D = 5
        with stage(nc, name, "split", "step", "summed", "added") as (block, s_split, step, s_summed, s_added):
            @block.vector
            def _(dve):
                link = Link(dve, step)
                link(dve.tensor_tensor(scaled[:], g, bc(dinv[:], H), ALU.mult))
                link(dve.tensor_copy(parts[:, :, 0, :], scaled[:]))
                link(dve.tensor_tensor(out, scaled[:], parts[:, :, 0, :], ALU.subtract))
                link(dve.tensor_copy(parts[:, :, 1, :], out))
                link(dve.tensor_tensor(out, out, parts[:, :, 1, :], ALU.subtract))
                dve.tensor_copy(parts[:, :, 2, :], out).then_inc(s_split, 1)
                dve.wait_ge(s_split, 1)
                dve.sem_inc(s_added, 1)
                with dve.Fori(0, NB // D) as i:
                    for j in range(D):
                        dve.wait_ge(s_summed, i * D + (j + 1))
                        o = out[:, bass.ds(i * D + j, 1), :].rearrange("p o f -> p (o f)")
                        dve.tensor_reduce(o, ps[:, j, 0:3 * H].rearrange("p (k f) -> p f k", f=H), AX, ALU.add
                                          ).then_inc(s_added, 1)

            @block.tensor
            def _(pe):
                pe.wait_ge(s_split, 1)
                with pe.Fori(0, NB // D) as i:
                    for j in range(D):
                        pe.wait_ge(s_added, i * D + 1)
                        for s in range(NB):
                            ins = pe.matmul(ps[:, j, 0:3 * H], C[:, s, bass.ds(i * (D * P) + j * P, P)],
                                            parts[:, s].rearrange("p k f -> p (k f)"),
                                            start=(s == 0), stop=(s == NB - 1))
                        ins.then_inc(s_summed, 1)
        self.recount(name + "_again", out)
        with stage(nc, name + "_own", "step") as (block, step):
            @block.vector
            def _(dve):
                link = Link(dve, step)
                link(dve.tensor_tensor(out, out, scaled[:], ALU.add))
                link(dve.tensor_tensor(out, out, bc(dinv[:], H), ALU.mult))

    def recount(self, name, out):
        nc, ps, c = self.nc, self.ps, self.c
        with ExitStack() as ctx:
            m = Memory(nc, ctx)
            rec = m.sb(f"{name}_rec", [P, RING, 2, 4])
            rows = m.sb(f"{name}_rows", [P, RING, 2, H])
            hot = m.sb(f"{name}_hot", [P, 2, 2, P])
            with stage(nc, name, "table", "clear", "hot", "summed", "added", "passed",
                       *[f"rec{k}" for k in range(RING)], *[f"row{k}" for k in range(RING)]) as (
                    block, s_table, s_clear, s_hot, s_summed, s_added, s_passed, *dmas):
                arrived, gathered = dmas[:RING], dmas[RING:]

                def needed(eng):
                    return eng.If(eng.value_load(self.many[0:1, 0:1], min_val=0, max_val=1) > 0)

                @block.sync
                def _(sp):
                    with needed(sp):
                        sp.dma_start(self.table.rearrange("(b p) w -> p b w", p=P), self.scaled[:]).then_inc(s_table, 16)
                        load_records(rec, self.rec_dram, arrived, [s_hot, s_summed])(sp)

                @block.gpsimd
                def _(pool):
                    with needed(pool):
                        pool.wait_ge(s_table, 16)
                        gather_rows(rec, R2_SRC, self.table, rows, arrived, gathered, s_summed, s_passed)(pool)

                @block.vector
                def _(dve):
                    def one_hot(u, k, rnd, b):
                        dve.wait_ge(arrived[k], rnd * 16 + 16)
                        if reused(u, 2):
                            dve.wait_ge(s_summed, u - 1)
                        for j in range(2):
                            ins = dve.tensor_scalar(hot[:, k % 2, j, :], c["iota"][:], rec[:, k, j, R2_LOC:R2_LOC + 1],
                                                    None, ALU.is_equal)
                        ins.then_inc(s_hot, 1)

                    def add(u, k, rnd, b):
                        dve.wait_ge(s_summed, u + 1)
                        if reused(u, 1):
                            dve.wait_ge(s_added, u)
                        o = out[:, bass.ds(b, 1), :].rearrange("p o f -> p (o f)")
                        dve.tensor_tensor(o, o, ps[:, k % 2, 0:H], ALU.add).then_inc(s_added, 1)
                    with needed(dve):
                        dve.memset(out, 0.0).then_inc(s_clear, 1)
                        dve.wait_ge(s_clear, 1)
                        over_units(dve, [(0, one_hot), (1, add)], self.blocks)

                @block.tensor
                def _(pe):
                    def sums(u, k, rnd, b):
                        pe.wait_ge(s_hot, u + 1)
                        pe.wait_ge(gathered[k], rnd * 32 + 32)
                        if reused(u, 2):
                            pe.wait_ge(s_added, u - 1)
                        for j in range(2):
                            ins = pe.matmul(ps[:, k % 2, 0:H], hot[:, k % 2, j, :], rows[:, k, j, :],
                                            start=(j == 0), stop=(j == 1))
                        ins.then_inc(s_summed, 1)
                    with needed(pe):
                        over_units(pe, [(0, sums)])



def third_part(nc, m, x, h, tmp, spread):
    with ExitStack() as ctx:
        t = Memory(nc, ctx)
        start, moved = t.sb("start", [P, NB, H]), t.sb("moved", [P, NB, H])
        layer_norm(nc, "ln2", x[:], h[:], tmp[:], relu=True)
        with stage(nc, "start", "step") as (block, step):
            @block.vector
            def _(dve):
                dve.tensor_scalar(start[:], h[:], 0.8, None, ALU.mult)
        with nc.Fori(0, 5):
            spread("step", h[:], moved[:])
            with stage(nc, "blend", "step") as (block, step):
                @block.vector
                def _(dve):
                    dve.scalar_tensor_tensor(h[:], moved[:], 0.2, start[:], ALU.mult, ALU.add)
        with stage(nc, "res2", "step") as (block, step):
            @block.vector
            def _(dve):
                dve.tensor_tensor(x[:], x[:], h[:], ALU.add)



def batch_norm(nc, c, ps, name, y, sq, gain, bias, before=None, relu_before=False, relu_after=False, eps=1e-5):
    with ExitStack() as ctx:
        m = Memory(nc, ctx)
        mean, var = m.sb(f"{name}_mean", [P, H]), m.sb(f"{name}_var", [P, H])
        with stage(nc, name, "step", "ready", "summed", "root") as (block, step, s_ready, s_summed, s_root):
            @block.tensor
            def _(pe):
                for n, v in enumerate((y, sq)):
                    pe.wait_ge(s_ready, n + 1)
                    for b in range(NB):
                        ins = pe.matmul(ps[:, n, 0:H], c["ones"][:] if b < NB - 1 else c["some"][:], v[:, b, :],
                                        start=(b == 0), stop=(b == NB - 1))
                    ins.then_inc(s_summed, 1)

            @block.vector
            def _(dve):
                link = Link(dve, step)
                if before is not None:
                    link(dve.tensor_tensor(y, y, along(before, NB), ALU.add))
                if relu_before:
                    link(dve.tensor_scalar(y, y, 0.0, None, ALU.max))
                dve.sem_inc(s_ready, 1)
                dve.wait_ge(s_summed, 1)
                link(dve.tensor_scalar(mean[:], ps[:, 0, 0:H], 1.0 / N, None, ALU.mult))
                link(dve.tensor_tensor(y, y, along(mean[:], NB), ALU.subtract))
                dve.tensor_tensor(sq, y, y, ALU.mult).then_inc(s_ready, 1)
                dve.wait_ge(s_summed, 2)
                link(dve.tensor_scalar(var[:], ps[:, 1, 0:H], 1.0 / N, eps, ALU.mult, ALU.add))
                dve.wait_ge(s_root, 1)
                link(dve.reciprocal(var[:], var[:]))
                link(dve.tensor_tensor(var[:], var[:], gain, ALU.mult))
                link(dve.tensor_tensor(y, y, along(var[:], NB), ALU.mult))
                link(dve.tensor_tensor(y, y, along(bias, NB), ALU.add))
                if relu_after:
                    link(dve.tensor_scalar(y, y, 0.0, None, ALU.max))

            @block.scalar
            def _(act):
                act.wait_ge(step, (before is not None) + relu_before + 3)
                act.sqrt(var[:], var[:]).then_inc(s_root, 1)


def stream(nc, c, ps, name, x, w, out, spare, accumulate=False):
    K, k, f = w.shape
    per = 3 if k == 1 else 2
    groups = [range(b, min(b + per, NB)) for b in range(0, NB, per)]
    if True:
        xT = spare[0:K, 0:2 * k * per * P].rearrange("p (h i n) -> p h i n", h=2, i=k)
        with stage(nc, name, "turned", "copied", "summed", "out") as (block, s_turned, s_copied, s_summed, s_out):
            @block.tensor
            def _(pe):
                def turn_in(g):
                    if g >= 2:
                        pe.wait_ge(s_copied, (g - 1) * k)
                    for i in range(k):
                        for j, b in enumerate(groups[g]):
                            ins = pe.transpose(ps[0:K, 2 * (g % 2) + i, P * j:P * j + P], x[:, b, K * i:K * i + K],
                                               c["ident"][:])
                        ins.then_inc(s_turned, 1)

                def products(g):
                    pe.wait_ge(s_copied, (g + 1) * k)
                    if g >= 2:
                        pe.wait_ge(s_out, g - 1)
                    for j, b in enumerate(groups[g]):
                        for i in range(k):
                            ins = pe.matmul(ps[:, 4 + g % 2, f * j:f * j + f], xT[:, g % 2, i, P * j:P * j + P],
                                            w[:, i, :], start=(i == 0), stop=(i == k - 1))
                    ins.then_inc(s_summed, 1)
                for g in range(len(groups) + 1):
                    if g < len(groups):
                        turn_in(g)
                    if g:
                        products(g - 1)

            @block.scalar
            def _(act):
                for g, bs in enumerate(groups):
                    n = len(bs) * P
                    if g >= 2:
                        act.wait_ge(s_summed, g - 1)
                    for i in range(k):
                        act.wait_ge(s_turned, g * k + i + 1)
                        act.copy(xT[:, g % 2, i, 0:n], ps[0:K, 2 * (g % 2) + i, 0:n]).then_inc(s_copied, 1)

            @block.vector
            def _(dve):
                for g, bs in enumerate(groups):
                    dve.wait_ge(s_summed, g + 1)
                    o = out[:, bs[0]:bs[-1] + 1, :]
                    p = ps[:, 4 + g % 2, 0:f * len(bs)].rearrange("p (b f) -> p b f", f=f)
                    if accumulate:
                        dve.tensor_tensor(o, o, p, ALU.add).then_inc(s_out, 1)
                    else:
                        dve.tensor_copy(o, p).then_inc(s_out, 1)


def fourth_part(nc, c, m, ps, a, x, h, tmp, spread):
    kept = nc.dram_tensor("kept", [P, NB, H], F32).ap()
    te = nc.dram_tensor("time_rows", [1, C9 + C3], F32).ap()
    spare = x[:].rearrange("p b f -> p (b f)")
    w_in, wc1 = m.sb("w_in", [H, 1, C3]), m.sb("wc1", [FC, 2, H])
    wc2, w_out = m.sb("wc2", [H, 1, C3]), m.sb("w_out", [FC, 2, H])
    rows = m.sb("rows_now", [P, 3, H])
    columns = lambda v, j: v[:, :, bass.ds(j * H, H)]
    part = lambda v, j: v[bass.ds(j * H, H)].partition_broadcast(P)
    halves = lambda sb, dram: [(sb[:, i, :], dram[FC * i:FC * i + FC]) for i in range(2)]

    def norm(name, j, y, sq, names, more=(), **relus):
        send(nc, name + "_rows", [(rows[:, n, :], part(v, j)) for n, v in enumerate(names)] + list(more))
        batch_norm(nc, c, ps, name, y, sq, rows[:, 1, :], rows[:, 2, :], before=rows[:, 0, :], **relus)

    def move(name, to, what):
        with stage(nc, name) as (block,):
            @block.vector
            def _(dve):
                dve.tensor_copy(to, what)

    time_rows(nc, ps, a, te)
    te1, te2 = te[0, 0:C9], te[0, C9:]
    layer_norm(nc, "ln3", x[:], h[:], tmp[:], relu=True)
    send(nc, "load3", [(kept, x[:]), (w_in[:, 0, :], a["W_in"])] + halves(w_out, a["W_out"]))
    y = m.sb("wide", [P, NB, C3])
    spread("conv_in", h[:], tmp[:])
    stream(nc, c, ps, "in_w", tmp[:], w_in[:], y[:], spare)
    with nc.Fori(0, C3 // H) as j:
        norm("bn_in", j, columns(y[:], j), tmp[:], [a["b_in"], a["g_in"], a["be_in"]], relu_after=True)
        move("pick1", h[:], columns(y[:], j))
        spread("conv1", h[:], tmp[:])
        move("put1", columns(y[:], j), tmp[:])
    with ExitStack() as ctx:
        z = Memory(nc, ctx).sb("mixed", [P, NB, C3])
        with stage(nc, "clear_z") as (block,):
            @block.vector
            def _(dve):
                dve.memset(z[:], 0.0)
        with nc.Fori(0, C9 // H) as j:
            send(nc, "load_c", [(wc1[:, i, :], a["Wc1"][FC * i:FC * i + FC, bass.ds(j * H, H)]) for i in range(2)]
                 + [(wc2[:, 0, :], a["Wc2"][bass.ds(j * H, H), :])])
            stream(nc, c, ps, "c1_w", y[:], wc1[:], h[:], spare)
            norm("bn1", j, h[:], tmp[:], [te1, a["g1"], a["be1"]], relu_before=True)
            stream(nc, c, ps, "c2_w", h[:], wc2[:], z[:], spare, accumulate=True)
        move("keep_z", y[:], z[:])
    with nc.Fori(0, C3 // H) as j:
        move("pick2", h[:], columns(y[:], j))
        spread("conv2", h[:], tmp[:])
        norm("bn2", j, tmp[:], h[:], [te2, a["g2"], a["be2"]], relu_before=True)
        move("put2", columns(y[:], j), tmp[:])
    stream(nc, c, ps, "out_w", y[:], w_out[:], h[:], spare)
    spread("conv_out", h[:], tmp[:])
    norm("bn_out", 0, tmp[:], h[:], [a["b_out"], a["g_out"], a["be_out"]], more=[(x[:], kept)], relu_after=True)
    with stage(nc, "res3") as (block,):
        @block.vector
        def _(dve):
            dve.tensor_tensor(x[:], x[:], tmp[:], ALU.add)


def time_rows(nc, ps, a, te):
    with ExitStack() as ctx:
        m = Memory(nc, ctx)
        ang, turns, k, freq = (m.sb(f"time_{n}", [T, 1]) for n in ("ang", "turns", "k", "freq"))
        bias = m.sb("time_bias", [T, 1])
        wtm, wt = m.sb("time_wtm", [T, T]), m.sb("time_wt", [T, C9 + C3])
        bt, cb = m.sb("time_bt", [1, C9 + C3]), m.sb("time_cb", [1, C9 + C3])
        flat = lambda v: v.rearrange("(o f) -> o f", o=1)
        send(nc, "load_time", [(ang[:], a["timestep"].partition_broadcast(T)), (freq[:], a["freqs"]), (wtm[:], a["Wtm"]),
                               (wt[:, 0:C9], a["Wt1"]), (wt[:, C9:], a["Wt2"]),
                               (bias[:], a["btm"].rearrange("(p o) -> p o", o=1)),
                               (bt[:, 0:C9], flat(a["bt1"])), (bt[:, C9:], flat(a["bt2"])),
                               (cb[:, 0:C9], flat(a["bc1"])), (cb[:, C9:], flat(a["bc2"]))])
        with stage(nc, "time", "step", "sin", "mixed", "relu", "rows") as (block, step, s_sin, s_mixed, s_relu, s_rows):
            R = 12582912.0
            PI2 = (6.28125, float(np.float32(2 * math.pi - 6.28125)),
                   2 * math.pi - 6.28125 - float(np.float32(2 * math.pi - 6.28125)))

            @block.vector
            def _(dve):
                link = Link(dve, step)
                link(dve.tensor_tensor(ang[:], ang[:], freq[:], ALU.mult))
                link(dve.tensor_scalar(turns[:], ang[:], 0.5 / math.pi, None, ALU.mult))
                link(dve.tensor_scalar(turns[T // 2:, :], turns[T // 2:, :], 0.25, None, ALU.add))
                link(dve.tensor_scalar(k[:], turns[:], R, None, ALU.add))
                link(dve.tensor_scalar(k[:], k[:], -R, None, ALU.add))
                for part in PI2:
                    link(dve.scalar_tensor_tensor(ang[:], k[:], -part, ang[:], ALU.mult, ALU.add))
                link(dve.tensor_scalar(ang[T // 2:, :], ang[T // 2:, :], math.pi / 2, None, ALU.add))
                link(dve.tensor_scalar(ang[:], ang[:], 3.1415925, -3.1415925, ALU.min, ALU.max))
                dve.wait_ge(s_mixed, 1)
                link(dve.scalar_tensor_tensor(ang[:], ps[0:T, 0, 0:1], 1.0, bias[:], ALU.mult, ALU.add))
                dve.tensor_scalar(ang[:], ang[:], 0.0, None, ALU.max).then_inc(s_relu, 1)
                dve.wait_ge(s_rows, 1)
                link(dve.tensor_tensor(bt[:, 0:C9], bt[:, 0:C9], ps[0:1, 1, 0:C9], ALU.add))
                link(dve.tensor_tensor(bt[:, C9:], bt[:, C9:], ps[0:1, 2, 0:C3], ALU.add))
                link(dve.scalar_tensor_tensor(bt[:], bt[:], 0.0, cb[:], ALU.max, ALU.add))

            @block.scalar
            def _(act):
                act.wait_ge(step, 10)
                act.activation(turns[:], ang[:], ACT.Sin).then_inc(s_sin, 1)

            @block.tensor
            def _(pe):
                pe.wait_ge(s_sin, 1)
                pe.matmul(ps[0:T, 0, 0:1], wtm[:], turns[:], start=True, stop=True).then_inc(s_mixed, 1)
                pe.wait_ge(s_relu, 1)
                pe.matmul(ps[0:1, 1, 0:C9], ang[:], wt[:, 0:C9], start=True, stop=True)
                pe.matmul(ps[0:1, 2, 0:C3], ang[:], wt[:, C9:], start=True, stop=True).then_inc(s_rows, 1)
        send(nc, "time_out", [(te, bt[:])])


def network(nc, m, ps, a, o, upto=None):
    c = constants(nc, m)
    filled = nc.alloc_semaphore("filled")
    out_done = nc.alloc_semaphore("out_done")
    rec1 = nc.dram_tensor("edges_by_src", [SLOTS + P * (TW - TILES + 1), REC], F32).ap()
    rec2 = nc.dram_tensor("edges_by_dst", [SLOTS + P * (TW - TILES + 1), 4], F32).ap()
    blocks1, blocks2 = m.sb("blocks1", [P, BODIES + 1], I32), m.sb("blocks2", [P, BODIES + 1], I32)
    starts1, starts2 = m.sb("starts1", [P, NB + 1], I32), m.sb("starts2", [P, NB + 1], I32)
    x, h, tmp = (m.sb(f"nodes_{k}", [P, NB, H]) for k in "xht")

    with ExitStack() as ctx:
        t = Memory(nc, ctx)
        big = t.sb("big", [P, 2 * TW * NB + NB])
        n_filled = prefill(nc, t, [("rec1", rec1, REC, R_LOC), ("rec2", rec2, 4, R2_LOC)], filled)
        pos = t.sb("pos", [P, TW], U32)
        loc = t.sb("loc", [P, TW])
        group(nc, c, ps, "by_src", a["src"], big, pos[:], loc[:], blocks1[:], starts1[:])
        meta1 = big[:, 0:4 * TW].rearrange("p (t w) -> p t w", w=4)
        with ExitStack() as ctx2:
            t2 = Memory(nc, ctx2)
            cut, far = t2.sb("cut", [P, TW]), t2.sb("far", [P, TW])
            half_pi = t2.sb("half_pi", [P, 1])
            with stage(nc, "cutoff", "in", "step", "cos") as (block, s_in, step, cos):
                @block.sync
                def _(sp):
                    sp.dma_start(cut[:], a["ew"]).then_inc(s_in, 16)

                @block.vector
                def _(dve):
                    link = Link(dve, step)
                    dve.memset(half_pi[:], math.pi / 2)
                    dve.memset(meta1[:, :, 0:2], 0.0)
                    dve.tensor_copy(meta1[:, :, 3], loc[:])
                    dve.wait_ge(s_in, 16)
                    link(dve.tensor_scalar(far[:], cut[:], 6.0, None, ALU.is_lt))
                    link(dve.tensor_scalar(cut[:], cut[:], 6.0, -6.0, ALU.min, ALU.max))
                    link(dve.scalar_tensor_tensor(cut[:], cut[:], -1.0, cut[:], ALU.mult, ALU.max))
                    dve.wait_ge(cos, 1)
                    link(dve.tensor_scalar(cut[:], cut[:], 1.0, 0.5, ALU.add, ALU.mult))
                    link(dve.tensor_tensor(meta1[:, :, 0], cut[:], far[:], ALU.mult))

                @block.scalar
                def _(act):
                    act.wait_ge(step, 3)
                    act.activation(cut[:], cut[:], ACT.Sin, bias=half_pi[:], scale=-math.pi / 6).then_inc(cos, 1)
        with ExitStack() as ctx2:
            t2 = Memory(nc, ctx2)
            end = t2.sb("end", [P, TW], I32)
            send(nc, "load_dst", [(end[:], a["dst"]), (x[:], a["xin"])])
            with stage(nc, "meta1_dst", "step") as (block, step):
                @block.vector
                def _(dve):
                    dve.tensor_copy(meta1[:, :, 2].bitcast(I32), end[:])
        scatter(nc, "scatter1", meta1, pos, rec1, REC, a["ea"], filled, n_filled)
        group(nc, c, ps, "by_dst", a["dst"], big, pos[:], loc[:], blocks2[:], starts2[:])
        weight, start = big[:, 4 * TW:5 * TW], big[:, 5 * TW:6 * TW].bitcast(I32)
        send(nc, "load_meta2", [(weight, a["ew1"]), (start, a["src"])])
        with stage(nc, "meta2", "step") as (block, step):
            @block.vector
            def _(dve):
                dve.tensor_copy(meta1[:, :, R2_W1], weight)
                dve.tensor_copy(meta1[:, :, R2_SRC].bitcast(I32), start)
                dve.tensor_copy(meta1[:, :, R2_LOC], loc[:])
                dve.memset(meta1[:, :, 3], 0.0)
        scatter(nc, "scatter2", meta1, pos, rec2, 4, None, filled, n_filled)
    with ExitStack() as ctx:
        acc = first_part(nc, c, Memory(nc, ctx), ps, a, x, h, tmp, rec1, blocks1, upto)
        if upto in ("gate", "attend"):
            return debug(nc, o, acc[:], out_done)
    if upto == "L0":
        return debug(nc, o, x[:], out_done)
    with ExitStack() as ctx:
        second_part(nc, c, Memory(nc, ctx), ps, x, h, tmp, rec2, blocks2)
    if upto == "L1":
        return debug(nc, o, x[:], out_done)
    dinv = m.sb("dinv", [P, NB])
    many = m.sb("many", [P, 1], I32)
    C = m.sb("C", [P, NB, NP], BF16)
    with ExitStack() as ctx:
        count_edges(nc, Memory(nc, ctx), ps, rec1, starts1, C)
    degrees(nc, c, m, ps, C, dinv, many)
    spread = Spread(nc, c, ps, C, dinv, many, rec2, blocks2)
    third_part(nc, m, x, h, tmp, spread)
    if upto == "L2":
        return debug(nc, o, x[:], out_done)
    fourth_part(nc, c, m, ps, a, x, h, tmp, spread)
    with stage(nc, "result") as (block,):
        @block.sync
        def _(sp):
            sp.dma_start(o["y"], x[:]).then_inc(out_done, 16)
            sp.wait_ge(out_done, 16)


def debug(nc, o, what, sem):
    with stage(nc, "dbg") as (block,):
        @block.sync
        def _(sp):
            sp.dma_start(o["y"][:, :, 0:what.shape[2]], what).then_inc(sem, 16)
            sp.wait_ge(sem, 16)


def freqs():
    half = T // 2
    f = np.exp(np.arange(half, dtype=np.float32) * np.float32(-math.log(10000.0) / (half - 1)))
    return np.concatenate([f, f]).astype(np.float32).reshape(T, 1)


def kernel(**inputs):
    import concourse.bacc as bacc
    from concourse.bass_utils import run_bass_kernel_spmd

    v = {k: np.asarray(x) for k, x in inputs.items()}

    def per_edge(x, pad):
        out = np.full((EP,) + x.shape[1:], pad, x.dtype)
        out[:E] = x
        return np.ascontiguousarray(out.reshape(TW, P, *x.shape[1:]).swapaxes(0, 1))

    def per_node(x):
        out = np.zeros((NP,) + x.shape[1:], x.dtype)
        out[:N] = x
        return np.ascontiguousarray(out.reshape(NB, P, *x.shape[1:]).swapaxes(0, 1))

    arrays = {
        "src": per_edge(v["src"], NP), "dst": per_edge(v["dst"], NP), "ea": per_edge(v["edge_attr_40"], 0),
        "ew": per_edge(v["edge_weight"], 0), "ew1": per_edge(v["edge_weight1"][:, 0], 0),
        "xin": per_node(v["x"]), "node_type": per_node(v["node_type_119"]), "node_vec": per_node(v["node_vec"]),
        "freqs": freqs(),
    }
    for k in v:
        if k.startswith(("L0_gnn_", "L3_gnn_")):
            arrays[k[7:]] = np.ascontiguousarray(v[k])

    nc = bacc.Bacc("TRN2", target_bir_lowering=False, num_devices=1)
    a = {k: nc.dram_tensor(k, x.shape, mybir.dt.from_np(x.dtype), kind="ExternalInput").ap() for k, x in arrays.items()}
    o = {"y": nc.dram_tensor("y", (P, NB, H), F32, kind="ExternalOutput").ap()}
    with ExitStack() as ctx:
        network(nc, Memory(nc, ctx), ctx.enter_context(nc.psum_tensor("banks", [P, 8, 512], F32)), a, o)
    r = run_bass_kernel_spmd(nc, [arrays], core_ids=[0])
    y = np.asarray(r.results[0]["y"])
    return y.transpose(1, 0, 2).reshape(NP, H)[:N]
```

```python
import math
from contextlib import ExitStack, contextmanager

import numpy as np

import concourse.bass as bass
from concourse import mybir
from concourse.alu_op_type import AluOpType as ALU

ACT = mybir.ActivationFunctionType
F32 = mybir.dt.float32
BF16 = mybir.dt.bfloat16
I32 = mybir.dt.int32
I16 = mybir.dt.int16
U32 = mybir.dt.uint32
AX = mybir.AxisListType.X

P = 128
N, E, H, RBF, LAYERS, G = 3125, 100000, 48, 40, 4, 32
NB = -(-N // P)
NP = NB * P
LAST = N - (NB - 1) * P
TILES = -(-E // P)
TW = -(-TILES // 16) * 16
EP = TW * P
UNIT = 2 * P
RING = 8
UNITS = -(-(E // UNIT + NB) // RING) * RING
BODIES = UNITS // RING
LEAST = E // (UNIT * RING)
LAG = 5
SLOTS = UNITS * UNIT
DUMP = SLOTS
REC = 44
R_CW, R_W1, R_DST, R_LOC = 40, 41, 42, 43
R2_W1, R2_SRC, R2_LOC = 0, 1, 2
BIG = float(2 ** 100)
NOMAX = float(2 ** 99)
C3, C9, T = 144, 432, 128
FC = 72
MC = 108
TAB0 = -(-(H + G + 1) // 4) * 4
TAB = -(-(2 * H + 2) // 4) * 4
TAB1 = -(-(H + 1) // 4) * 4


class Link:

    def __init__(self, eng, sem):
        self.eng, self.sem, self.n = eng, sem, 0

    def __call__(self, ins):
        self.n += 1
        ins.then_inc(self.sem, 1)
        self.eng.wait_ge(self.sem, self.n)


@contextmanager
def stage(nc, name, *sems):
    handles = [nc.alloc_semaphore(f"{name}_{s}") for s in sems]
    with nc.Block(name) as block:
        yield (block, *handles)
    nc.clear_and_free_semaphores(handles)
    nc.all_engine_barrier()


class Memory:

    def __init__(self, nc, ctx):
        self.nc, self.ctx = nc, ctx

    def sb(self, name, shape, dt=F32):
        return self.ctx.enter_context(self.nc.sbuf_tensor(f"sb_{name}", shape, dt))


def bc(ap, n):
    return ap.unsqueeze(2).to_broadcast([ap.shape[0], ap.shape[1], n])


def along(ap, n):
    return ap.unsqueeze(1).to_broadcast([ap.shape[0], n, ap.shape[1]])


def split(link, x, rest, parts):
    dve = link.eng
    link(dve.tensor_copy(parts[0], x))
    link(dve.tensor_tensor(rest, x, parts[0], ALU.subtract))
    link(dve.tensor_copy(parts[1], rest))
    link(dve.tensor_tensor(rest, rest, parts[1], ALU.subtract))
    link(dve.tensor_copy(parts[2], rest))



def constants(nc, m, tri):
    c = {
        "iota": m.sb("iota_f32", [P, P]), "iota16": m.sb("iota_i16", [P, P], I16), "part": m.sb("iota_part", [P, 1]),
        "ident": m.sb("ident_f32", [P, P]), "identb": m.sb("ident_bf16", [P, P], BF16),
        "tri": tri, "ones": m.sb("ones_f32", [P, P]),
        "some": m.sb("ones_last", [P, P]), "onesb": m.sb("ones_bf16", [P, P], BF16),
    }
    with stage(nc, "const", "made", "written") as (block, made, written):
        @block.gpsimd
        def _(pool):
            pool.iota(c["iota"][:], [[1, P]], base=0, channel_multiplier=0, allow_small_or_imprecise_dtypes=True)
            pool.iota(c["iota16"][:], [[1, P]], base=0, channel_multiplier=0)
            pool.iota(c["part"][:], [[0, 1]], base=0, channel_multiplier=1,
                      allow_small_or_imprecise_dtypes=True).then_inc(made, 1)

        @block.vector
        def _(dve):
            dve.memset(c["ones"][:], 1.0)
            dve.memset(c["onesb"][:], 1.0)
            dve.wait_ge(made, 1)
            dve.tensor_scalar(c["some"][:], c["part"][:].to_broadcast([P, P]), float(LAST), None, ALU.is_lt)
            dve.tensor_scalar(c["ident"][:], c["iota"][:], c["part"][:, 0:1], None, ALU.is_equal)
            dve.tensor_scalar(c["identb"][:], c["iota"][:], c["part"][:, 0:1], None, ALU.is_equal)
            dve.tensor_scalar(c["tri"][:], c["iota"][:], c["part"][:, 0:1], None, ALU.is_gt)
    return c



def group(nc, c, ps, name, key_dram, big, pos, loc, blocks, starts, beside=None):
    W3 = TW * NB
    onehot = big[:, 0:W3 // 2].bitcast(BF16).rearrange("p (t b) -> p t b", b=NB)
    within = big[:, W3 // 2:W3].bitcast(BF16).rearrange("p (t b) -> p t b", b=NB)
    before = big[:, W3:2 * W3 + NB].rearrange("p (t b) -> p t b", b=NB)
    with ExitStack() as ctx:
        m = Memory(nc, ctx)
        key = m.sb(f"{name}_key", [P, TW], I32)
        hi = m.sb(f"{name}_hi", [P, TW], I32)
        rank = m.sb(f"{name}_rank", [P, TW])
        one = m.sb(f"{name}_one", [P, TW])
        cnt = m.sb(f"{name}_cnt", [P, NB])
        cnti = m.sb(f"{name}_cnti", [P, NB], I32)
        cntu = m.sb(f"{name}_cntu", [P, NB], I32)
        units = m.sb(f"{name}_units", [P, NB])
        start = m.sb(f"{name}_start", [P, NB + 1])
        uid = m.sb(f"{name}_uid", [P, UNITS])
        blk = m.sb(f"{name}_blk", [P, LAG + UNITS + RING])
        step = m.sb(f"{name}_step", [P, UNITS + RING + LAG - 1])
        word = m.sb(f"{name}_word", [P, BODIES + 1])
        dump = m.sb(f"{name}_dump", [P, TW - TILES + 1])
        STEP = 16
        with stage(nc, name, "key", "made", "onehot", "counted", "copied_w", "copied_s", "done",
                   *Scatter.SEMS) as (block, s_key, s_made, s_onehot, s_counted, s_w, s_s, s_done, *others):
            @block.sync
            def _(sp):
                sp.dma_start(key[:], key_dram).then_inc(s_key, 16)
                if beside is not None:
                    beside.load(sp, *others)

            @block.gpsimd
            def _(pool):
                pool.iota(uid[:], [[1, UNITS]], base=0, channel_multiplier=0, allow_small_or_imprecise_dtypes=True)
                pool.iota(dump[:], [[P, TW - TILES + 1]], base=DUMP, channel_multiplier=1,
                          allow_small_or_imprecise_dtypes=True).then_inc(s_made, 1)
                if beside is not None:
                    beside.store(pool, *others)

            @block.tensor
            def _(pe):
                pe.wait_ge(s_onehot, 1)
                for j in range(TW // STEP):
                    if j >= 4:
                        pe.wait_ge(s_w, j - 3)
                        pe.wait_ge(s_s, j - 3)
                    oh = onehot[:, STEP * j:STEP * j + STEP, :]
                    pe.matmul(ps[:, 2 * (j % 4), 0:STEP * NB], c["tri"][:], oh, start=True, stop=True)
                    pe.matmul(ps[:, 2 * (j % 4) + 1, 0:STEP * NB], c["onesb"][:], oh, start=True,
                              stop=True).then_inc(s_counted, 1)

            @block.scalar
            def _(act):
                for j in range(TW // STEP):
                    act.wait_ge(s_counted, j + 1)
                    act.copy(within[:, STEP * j:STEP * j + STEP, :],
                             ps[:, 2 * (j % 4), 0:STEP * NB].rearrange("p (t b) -> p t b", b=NB)).then_inc(s_w, 1)

            @block.vector
            def _(dve):
                link = Link(dve, s_done)
                dve.memset(one[:], 1.0)
                dve.memset(before[:, 0:1, :], 0.0)
                dve.wait_ge(s_key, 16)
                link(dve.tensor_scalar(hi[:], key[:], 7, None, ALU.arith_shift_right))
                dve.wait_ge(s_made, 1)
                dve.tensor_tensor(onehot, bc(hi[:], NB), along(uid[:, 0:NB], TW), ALU.is_equal).then_inc(s_onehot, 1)
                link(dve.tensor_scalar(key[:], key[:], 127, None, ALU.bitwise_and))
                link(dve.tensor_copy(loc, key[:]))
                for j in range(TW // STEP):
                    dve.wait_ge(s_counted, j + 1)
                    dve.tensor_copy(before[:, STEP * j + 1:STEP * j + STEP + 1, :],
                                    ps[:, 2 * (j % 4) + 1, 0:STEP * NB].rearrange("p (t b) -> p t b", b=NB)
                                    ).then_inc(s_s, 1)
                dve.wait_ge(s_s, TW // STEP)
                for b in range(NB):
                    ins = dve.tensor_tensor_scan(before[:, 1:TW + 1, b], one[:], before[:, 1:TW + 1, b], 0.0,
                                                 ALU.mult, ALU.add)
                link(ins)
                link(dve.tensor_scalar(cnt[:], before[:, TW, :], float(UNIT - 1), None, ALU.add))
                link(dve.tensor_copy(cnti[:], cnt[:]))
                link(dve.tensor_scalar(cntu[:], cnti[:], 8, None, ALU.arith_shift_right))
                link(dve.tensor_copy(units[:], cntu[:]))
                link(dve.tensor_scalar(units[:], units[:], 1.0, None, ALU.max))
                link(dve.memset(start[:, 0:1], 0.0))
                link(dve.tensor_tensor_scan(start[:, 1:NB + 1], one[:, 0:NB], units[:], 0.0, ALU.mult, ALU.add))
                link(dve.tensor_copy(starts[:, 0:NB + 1], start[:]))
                link(dve.tensor_scalar(cnt[:, 0:1], start[:, NB:NB + 1], float(RING - 1 - LEAST * RING), None,
                                       ALU.add))
                link(dve.tensor_copy(cnti[:, 0:1], cnt[:, 0:1]))
                link(dve.tensor_scalar(starts[:, NB + 1:NB + 2], cnti[:, 0:1], RING.bit_length() - 1, None,
                                       ALU.arith_shift_right))
                link(dve.tensor_scalar(cnt[:], start[:, 0:NB], float(UNIT), None, ALU.mult))
                dve.wait_ge(s_w, TW // STEP)
                link(dve.tensor_tensor(before[:, 0:TW, :], before[:, 0:TW, :], within, ALU.add))
                link(dve.tensor_tensor(before[:, 0:TW, :], before[:, 0:TW, :], along(cnt[:], TW), ALU.add))
                link(dve.tensor_tensor(before[:, 0:TW, :], before[:, 0:TW, :], onehot, ALU.mult))
                link(dve.tensor_reduce(rank[:], before[:, 0:TW, :], AX, ALU.add))
                first = E - (TILES - 1) * P
                for a in range(first, P, 32):
                    link(dve.tensor_copy(rank[a:a + 32, TILES - 1:TILES], dump[a:a + 32, 0:1]))
                link(dve.tensor_copy(rank[:, TILES:TW], dump[:, 1:TW - TILES + 1]))
                link(dve.tensor_copy(pos, rank[:]))
                ge = big[:, 0:UNITS * NB].rearrange("p (u b) -> p u b", b=NB)
                link(dve.memset(blk[:, 0:LAG], 0.0))
                link(dve.tensor_tensor(ge, bc(uid[:], NB), along(start[:, 0:NB], UNITS), ALU.is_ge))
                link(dve.tensor_reduce(blk[:, LAG:LAG + UNITS], ge, AX, ALU.add))
                link(dve.tensor_scalar(blk[:, LAG:LAG + UNITS], blk[:, LAG:LAG + UNITS], -1.0, None, ALU.add))
                link(dve.memset(blk[:, LAG + UNITS:], float(NB - 1)))
                link(dve.tensor_tensor(step[:], blk[:, 1:], blk[:, 0:UNITS + RING + LAG - 1], ALU.subtract))
                first = blk[:, 0:UNITS + RING].rearrange("p (i k) -> p i k", k=RING)[:, :, 0]
                link(dve.tensor_scalar(word[:], first, 0.0, None, ALU.add))
                for k in range(RING + LAG - 1):
                    s = step[:, k:k + UNITS + 1:RING]
                    link(dve.scalar_tensor_tensor(word[:], s, float(32 << k), word[:], ALU.mult, ALU.add))
                link(dve.tensor_copy(blocks, word[:]))


def prefill(nc, memory, lists, sem):
    TIMES = 16
    with stage(nc, "prefill", "made") as (block, made):
        pads, at = [], 0
        for _, width, _ in lists:
            n = SLOTS // P // TIMES * width
            pads.append(memory[:, at:at + n].rearrange("p (r w) -> p r w", w=width))
            at += n

        @block.vector
        def _(dve):
            link = Link(dve, made)
            for pad, (_, _, place) in zip(pads, lists):
                link(dve.memset(pad, 0.0))
                link(dve.memset(pad[:, :, place:place + 1], -1.0))

        @block.sync
        def _(sp):
            sp.wait_ge(made, 2 * len(lists))
            for pad, (dram, _, _) in zip(pads, lists):
                view = dram[0:SLOTS, :].rearrange("(p i r) w -> p i r w", p=P, i=TIMES)
                for j in range(TIMES):
                    sp.dma_start(view[:, j], pad).then_inc(sem, 16)
    return 16 * TIMES * len(lists)


class Scatter:
    SEMS = ("in0", "in1", "sent0", "sent1", "passed")
    HALF = 8

    def __init__(self, m, name, meta_dram, pos_dram, rec_dram, width, feat_dram, filled, filled_n):
        self.meta, self.pos, self.list, self.feat, self.width = meta_dram, pos_dram, rec_dram, feat_dram, width
        self.filled, self.filled_n = filled, filled_n
        self.rec = m.sb(f"{name}_rec", [P, 2, self.HALF, width])
        self.idx = m.sb(f"{name}_idx", [P, 2, self.HALF], U32)

    def load(self, sp, in0, in1, sent0, sent1, passed):
        HALF, landed, sent = self.HALF, (in0, in1), (sent0, sent1)
        nf = self.width - self.meta.shape[2]

        def body(i):
            for h in range(2):
                at = bass.ds(i * (2 * HALF) + h * HALF, HALF)
                if not isinstance(i, int):
                    sp.wait_ge(sent[h], i * (16 * HALF))
                if nf:
                    sp.dma_start(self.rec[:, h, :, 0:nf], self.feat[:, at, :]).then_inc(landed[h], 16)
                sp.dma_start(self.rec[:, h, :, nf:], self.meta[:, at, :]).then_inc(landed[h], 16)
                sp.dma_start(self.idx[:, h, :], self.pos[:, at]).then_inc(landed[h], 16)
        body(0)
        with sp.Fori(1, TW // (2 * HALF)) as i:
            body(i)

    def store(self, pool, in0, in1, sent0, sent1, passed):
        HALF, landed, sent = self.HALF, (in0, in1), (sent0, sent1)
        per = 16 * (3 if self.width > self.meta.shape[2] else 2)
        pool.wait_ge(self.filled, self.filled_n)

        def body(i):
            for h in range(2):
                pool.wait_ge(landed[h], i * per + per)
                pool.sem_inc(passed, 1)
                for j in range(HALF):
                    pool.indirect_dma_start(self.list, bass.IndirectOffsetOnAxis(self.idx[:, h, j:j + 1], 0),
                                            self.rec[:, h, j, :], None).then_inc(sent[h], 16)
        body(0)
        with pool.Fori(1, TW // (2 * HALF)) as i:
            body(i)
        for h in range(2):
            pool.wait_ge(sent[h], 16 * HALF * (TW // (2 * HALF)))



def layer_norm(nc, name, x, out, tmp, gain=None, bias=None, relu=False, eps=1e-5):
    f = x.shape[2]
    with ExitStack() as ctx:
        m = Memory(nc, ctx)
        mean = m.sb(f"{name}_mean", [P, NB])
        var = m.sb(f"{name}_var", [P, NB])
        std = m.sb(f"{name}_std", [P, NB])
        with stage(nc, name, "step", "var", "std") as (block, step, s_var, s_std):
            @block.vector
            def _(dve):
                link = Link(dve, step)
                link(dve.tensor_reduce(mean[:], x, AX, ALU.add))
                link(dve.tensor_scalar(mean[:], mean[:], 1.0 / f, None, ALU.mult))
                link(dve.tensor_tensor(out, x, bc(mean[:], f), ALU.subtract))
                link(dve.tensor_tensor(tmp, out, out, ALU.mult))
                link(dve.tensor_reduce(var[:], tmp, AX, ALU.add))
                dve.tensor_scalar(var[:], var[:], 1.0 / f, eps, ALU.mult, ALU.add).then_inc(s_var, 1)
                dve.wait_ge(s_std, 1)
                link(dve.reciprocal(std[:], std[:]))
                link(dve.tensor_tensor(out, out, bc(std[:], f), ALU.mult))
                if gain is not None:
                    link(dve.tensor_tensor(out, out, along(gain, NB), ALU.mult))
                    link(dve.tensor_tensor(out, out, along(bias, NB), ALU.add))
                if relu:
                    link(dve.tensor_scalar(out, out, 0.0, None, ALU.max))

            @block.scalar
            def _(act):
                act.wait_ge(s_var, 1)
                act.sqrt(std[:], var[:]).then_inc(s_std, 1)


def turn(nc, c, ps, name, x, xT):
    f = x.shape[2]
    with stage(nc, name, "turned", "copied") as (block, turned, copied):
        groups = [range(b, min(b + 4, NB)) for b in range(0, NB, 4)]

        @block.tensor
        def _(pe):
            for g, bs in enumerate(groups):
                for j, b in enumerate(bs):
                    ins = pe.transpose(ps[0:f, g, P * j:P * j + P], x[:, b, :], c["ident"][:])
                ins.then_inc(turned, 1)

        @block.scalar
        def _(act):
            for g, bs in enumerate(groups):
                act.wait_ge(turned, g + 1)
                n = len(bs) * P
                act.copy(xT[0:f, 4 * P * g:4 * P * g + n], ps[0:f, g, 0:n]).then_inc(copied, 1)


def times(nc, ps, name, xT, w, out):
    k, f = w.shape
    per = 5 if f <= 100 else 3
    groups = [range(b, min(b + per, NB)) for b in range(0, NB, per)]
    with stage(nc, name, "summed", "copied") as (block, summed, copied):
        @block.tensor
        def _(pe):
            for g, bs in enumerate(groups):
                if g >= 8:
                    pe.wait_ge(copied, g - 7)
                for j, b in enumerate(bs):
                    ins = pe.matmul(ps[:, g % 8, f * j:f * j + f], xT[0:k, P * b:P * b + P], w, start=True, stop=True)
                ins.then_inc(summed, 1)

        @block.scalar
        def _(act):
            for g, bs in enumerate(groups):
                act.wait_ge(summed, g + 1)
                act.copy(out[:, bs[0]:bs[-1] + 1, :],
                         ps[:, g % 8, 0:f * len(bs)].rearrange("p (b f) -> p b f", f=f)).then_inc(copied, 1)


def send(nc, name, pairs):
    with stage(nc, name, "landed") as (block, landed):
        @block.sync
        def _(sp):
            for dst, src in pairs:
                sp.dma_start(dst, src).then_inc(landed, 16)
            sp.wait_ge(landed, 16 * len(pairs))


def bodies_of(eng, walk):
    return eng.value_load(walk[1], min_val=0, max_val=BODIES - LEAST) + LEAST


def over_units(eng, pieces, walk, placed=False):
    words, _ = walk
    deepest = max(lag for lag, _ in pieces)

    def body(i, begin, end):
        of = {}
        if placed:
            word = eng.value_load(words[0:1, bass.ds(i, 1)], min_val=0, max_val=2 ** (5 + RING + LAG) - 1)
            of[-LAG] = eng.snap(word & 31).with_bounds(min_val=0, max_val=NB - 1)
            for k in range(1 - LAG, 0 if end else RING):
                of[k] = eng.snap(of[k - 1] + ((word >> (4 + LAG + k)) & 1)).with_bounds(min_val=0, max_val=NB - 1)
        for k in range(deepest if end else RING):
            for lag, piece in pieces:
                if (begin and k < lag) or (end and k >= lag):
                    continue
                rnd = i if k >= lag else i - 1
                piece(i * RING + (k - lag), (k - lag) % RING, rnd, of.get(k - lag))

    bodies = bodies_of(eng, walk)
    body(0, True, False)
    with eng.Fori(1, bodies) as i:
        body(i, False, False)
    if deepest:
        body(bodies, False, True)


def reused(u, ring):
    return not isinstance(u, int) or u >= ring


def load_records(rec, rec_dram, arrived, freed, walk):
    view = rec_dram[0:SLOTS, :].rearrange("(u j p) w -> u p j w", j=2, p=P)

    def program(sp):
        def piece(u, k, rnd, b):
            if reused(u, RING):
                for sem in freed:
                    sp.wait_ge(sem, u - RING + 1)
            src = view[bass.ds(u, 1)].rearrange("o p j w -> (o p) j w")
            sp.dma_start(rec[:, k, :, :], src).then_inc(arrived[k], 16)
        over_units(sp, [(0, piece)], walk)
    return program


def gather_rows(rec, word, table, rows, arrived, gathered, used, passed, walk):
    def program(pool):
        def piece(u, k, rnd, b):
            pool.wait_ge(arrived[k], rnd * 16 + 16)
            if reused(u, RING):
                pool.wait_ge(used, u - RING + 1)
            pool.sem_inc(passed, 1)
            for j in range(2):
                pool.indirect_dma_start(rows[:, k, j, :], None, table,
                                        bass.IndirectOffsetOnAxis(rec[:, k, j, word:word + 1].bitcast(U32), 0)
                                        ).then_inc(gathered[k], 16)
        over_units(pool, [(0, piece)], walk)
    return program


def gate_edges(nc, c, ps, name, rec_dram, table, embp, w, walk, acc):
    with ExitStack() as ctx:
        m = Memory(nc, ctx)
        rec = m.sb(f"{name}_rec", [P, RING, 2, REC])
        rows = m.sb(f"{name}_rows", [P, RING, 2, TAB0])
        hot = m.sb(f"{name}_hot", [P, RING, 2, P])
        attrT = m.sb(f"{name}_attrT", [RBF, 2, UNIT])
        hotT = m.sb(f"{name}_hotT", [P, 2, UNIT], BF16)
        hid = m.sb(f"{name}_hid", [64, 2, UNIT])
        prod = m.sb(f"{name}_prod", [P, 2, 3, G])
        dots = m.sb(f"{name}_dots", [P, 2])
        wgt = m.sb(f"{name}_wgt", [P, 2])
        msg = m.sb(f"{name}_msg", [P, 2, 2, H + 1])
        names = ["ones", "hot", "turned", "copied", "mixed", "silu", "gated", "msg", "summed", "added", "link", "passed"]
        with stage(nc, name, *names, *[f"rec{k}" for k in range(RING)], *[f"row{k}" for k in range(RING)]) as (
                block, s_ones, s_hot, s_turned, s_copied, s_mixed, s_silu, s_gated, s_msg, s_summed, s_added, s_link,
                s_passed, *dmas):
            arrived, gathered = dmas[:RING], dmas[RING:]
            block.sync(load_records(rec, rec_dram, arrived, [s_msg, s_turned], walk))
            block.gpsimd(gather_rows(rec, R_DST, table, rows, arrived, gathered, s_msg, s_passed, walk))

            hot_bank = ps[:, 0, UNIT:UNIT + P].bitcast(BF16)

            @block.tensor
            def _(pe):
                def turn_in(u, k, rnd, b):
                    pe.wait_ge(arrived[k], rnd * 16 + 16)
                    pe.wait_ge(s_hot, u + 1)
                    if reused(u, 1):
                        pe.wait_ge(s_copied, u * 2)
                    for j in range(2):
                        pe.transpose(hot_bank[:, P * j:P * j + P], hot[:, k, j, :].bitcast(BF16)[:, 1::2],
                                     c["identb"][:])
                    for j in range(2):
                        ins = pe.transpose(ps[0:RBF, 0, P * j:P * j + P], rec[:, k, j, 0:RBF], c["ident"][:])
                    ins.then_inc(s_turned, 1)

                def mix(u, k, rnd, b):
                    pe.wait_ge(s_copied, u * 2 + 2)
                    if reused(u, 1):
                        pe.wait_ge(s_silu, u)
                    if reused(u, 4):
                        pe.wait_ge(s_msg, u - 3)
                    for j in range(2):
                        pe.matmul(ps[:, 2 + k % 4, 128 + 3 * G * j:128 + 3 * G * (j + 1)],
                                  hotT[:, k % 2, P * j:P * j + P],
                                  embp[:, bass.ds(b, 1), :].rearrange("p o f -> p (o f)"), start=True, stop=True)
                    pe.matmul(ps[0:H, 1, 0:UNIT], w["F1W"][:], attrT[:, k % 2, :], start=True, stop=True
                              ).then_inc(s_mixed, 1)

                def gate(u, k, rnd, b):
                    pe.wait_ge(s_silu, u + 1)
                    for j in range(2):
                        ins = pe.matmul(ps[:, 2 + k % 4, H * j:H * j + H], hid[0:H + 1, k % 2, P * j:P * j + P],
                                        w["F2"][:], start=True, stop=True)
                    ins.then_inc(s_gated, 1)

                def total(u, k, rnd, b):
                    pe.wait_ge(s_msg, u + 1)
                    if reused(u, 2):
                        pe.wait_ge(s_added, u - 1)
                    for j in range(2):
                        ins = pe.matmul(ps[:, 6 + k % 2, 0:H + 1], hot[:, k, j, :], msg[:, k % 2, j, :],
                                        start=(j == 0), stop=(j == 1))
                    ins.then_inc(s_summed, 1)
                over_units(pe, [(3, gate), (2, mix), (1, turn_in), (4, total)], walk, True)

            @block.scalar
            def _(act):
                def copy_in(u, k, rnd, b):
                    act.wait_ge(s_turned, u + 1)
                    if reused(u, 2):
                        act.wait_ge(s_mixed, u - 1)
                    act.copy(attrT[:, k % 2, :], ps[0:RBF, 0, 0:UNIT]).then_inc(s_copied, 1)
                    act.copy(hotT[:, k % 2, :], hot_bank[:, 0:UNIT]).then_inc(s_copied, 1)

                def silu(u, k, rnd, b):
                    act.wait_ge(s_mixed, u + 1)
                    if reused(u, 1):
                        act.wait_ge(s_ones, 1)
                    if reused(u, 2):
                        act.wait_ge(s_gated, u - 1)
                    act.activation(hid[0:H, k % 2, :], ps[0:H, 1, 0:UNIT], ACT.Silu, bias=w["F1b"][:]
                                   ).then_inc(s_silu, 1)
                act.wait_ge(s_ones, 1)
                over_units(act, [(2, silu), (1, copy_in)], walk)

            @block.vector
            def _(dve):
                dve.memset(hid[:], 1.0).then_inc(s_ones, 1)

                def one_hot(u, k, rnd, b):
                    dve.wait_ge(arrived[k], rnd * 16 + 16)
                    if reused(u, RING):
                        dve.wait_ge(s_summed, u - RING + 1)
                    for j in range(2):
                        ins = dve.tensor_scalar(hot[:, k, j, :], c["iota"][:], rec[:, k, j, R_LOC:R_LOC + 1], None,
                                                ALU.is_equal)
                    ins.then_inc(s_hot, 1)

                def message(u, k, rnd, b):
                    dve.wait_ge(gathered[k], rnd * 32 + 32)
                    dve.wait_ge(s_gated, u + 1)
                    if reused(u, 2):
                        dve.wait_ge(s_summed, u - 1)
                    if reused(u, 1):
                        dve.wait_ge(s_msg, u)
                    base = u * 4
                    x = rows[:, k]
                    o = msg[:, k % 2]
                    dve.tensor_tensor(prod[:], ps[:, 2 + k % 4, 128:128 + 6 * G].rearrange("p (j i f) -> p j i f", i=3, f=G),
                                      x[:, :, H:H + G].unsqueeze(2).to_broadcast([P, 2, 3, G]), ALU.mult
                                      ).then_inc(s_link, 1)
                    dve.tensor_tensor(wgt[:], rec[:, k, :, R_CW], x[:, :, H + G], ALU.mult).then_inc(s_link, 1)
                    dve.wait_ge(s_link, base + 2)
                    dve.tensor_reduce(dots[:], prod[:].rearrange("p j i f -> p j (i f)"), AX, ALU.add).then_inc(s_link, 1)
                    dve.tensor_copy(o[:, :, H:H + 1], x[:, :, H + G:H + G + 1])
                    dve.wait_ge(s_link, base + 3)
                    for j in range(2):
                        ins = dve.scalar_tensor_tensor(o[:, j, 0:H], ps[:, 2 + k % 4, H * j:H * j + H],
                                                       dots[:, j:j + 1], x[:, j, 0:H], ALU.add, ALU.mult)
                    ins.then_inc(s_link, 1)
                    dve.wait_ge(s_link, base + 4)
                    dve.tensor_tensor(o[:, :, 0:H], o[:, :, 0:H], bc(wgt[:], H), ALU.mult).then_inc(s_msg, 1)

                def add(u, k, rnd, b):
                    dve.wait_ge(s_summed, u + 1)
                    if reused(u, 1):
                        dve.wait_ge(s_added, u)
                    a = acc[:, bass.ds(b, 1), :].rearrange("p o f -> p (o f)")
                    dve.tensor_tensor(a, a, ps[:, 6 + k % 2, 0:H + 1], ALU.add).then_inc(s_added, 1)
                over_units(dve, [(4, message), (5, add), (0, one_hot)], walk, True)


def attend(nc, c, ps, name, rec_dram, width, place, other, score, table, tab, at_h, queryT, walk, acc, nmax):
    with ExitStack() as ctx:
        m = Memory(nc, ctx)
        rec = m.sb(f"{name}_rec", [P, RING, 2, width])
        rows = m.sb(f"{name}_rows", [P, RING, 2, tab])
        out_of = m.sb(f"{name}_out_of", [P, 4, 2, P], F32 if score is not None else BF16)
        prob = m.sb(f"{name}_prob", [P, 2, UNIT])
        probT = m.sb(f"{name}_probT", [P, 2, UNIT])
        top = m.sb(f"{name}_top", [P, RING])
        ntop = m.sb(f"{name}_ntop", [P, RING])
        fall = m.sb(f"{name}_fall", [P, RING])
        shrink = m.sb(f"{name}_shrink", [P, RING])
        keyT = m.sb(f"{name}_keyT", [H + 1, 2, UNIT])
        query = m.sb(f"{name}_query", [H + 1, 2, P])
        names = ["key", "outof", "turned", "copied", "query", "scored", "maxed", "prob", "shrunk", "turnedp", "copiedp",
                 "summed", "added", "biased", "linka", "linkb", "passed", "passedpe"]
        with stage(nc, name, *names, *[f"rec{k}" for k in range(RING)], *[f"row{k}" for k in range(RING)]) as (
                block, s_key, s_outof, s_turned, s_copied, s_query, s_scored, s_maxed, s_prob, s_shrunk, s_turnedp,
                s_copiedp, s_summed, s_added, s_biased, s_linka, s_linkb, s_passed, s_passed_pe, *dmas):
            arrived, gathered = dmas[:RING], dmas[RING:]
            block.sync(load_records(rec, rec_dram, arrived, [s_biased, s_summed] if score is not None else [s_key, s_outof],
                                    walk))
            block.gpsimd(gather_rows(rec, other, table, rows, arrived, gathered, s_summed, s_passed, walk))

            @block.tensor
            def _(pe):
                def turn_keys(u, k, rnd, b):
                    pe.wait_ge(s_key, u + 1)
                    if reused(u, 2):
                        pe.wait_ge(s_copied, u - 1)
                    pe.sem_inc(s_passed_pe, 1)
                    for j in range(2):
                        ins = pe.transpose(ps[0:H + 1, k % 2, P * j:P * j + P], rows[:, k, j, 0:H + 1], c["ident"][:])
                    ins.then_inc(s_turned, 1)

                def scores(u, k, rnd, b):
                    if reused(u, 2):
                        pe.wait_ge(s_prob, u - 1)
                    bank = ps[:, 2 + k % 2, :]
                    if score is not None:
                        pe.wait_ge(s_biased, u + 1)
                        for j in range(2):
                            ins = pe.transpose(bank[:, P * j:P * j + P], out_of[:, k % 4, j, :], c["ident"][:])
                    else:
                        pe.wait_ge(s_copied, u + 1)
                        pe.wait_ge(s_query, u + 1)
                        pe.wait_ge(s_outof, u + 1)
                        pe.matmul(bank[:, 0:UNIT], query[:, k % 2, :], keyT[:, k % 2, :], start=True, stop=False)
                        for j in range(2):
                            ins = pe.matmul(bank[:, P * j:P * j + P], out_of[:, k % 4, j, :], c["identb"][:],
                                            start=False, stop=(j == 1))
                    ins.then_inc(s_scored, 1)

                def turn_probs(u, k, rnd, b):
                    pe.wait_ge(s_prob, u + 1)
                    if reused(u, 2):
                        pe.wait_ge(s_copiedp, u - 1)
                    for j in range(2):
                        ins = pe.transpose(ps[:, 4 + k % 2, P * j:P * j + P], prob[:, k % 2, P * j:P * j + P],
                                           c["ident"][:])
                    ins.then_inc(s_turnedp, 1)

                def sums(u, k, rnd, b):
                    pe.wait_ge(s_copiedp, u + 1)
                    if score is not None:
                        pe.wait_ge(gathered[k], rnd * 32 + 32)
                    if reused(u, 2):
                        pe.wait_ge(s_added, u - 1)
                    for j in range(2):
                        ins = pe.matmul(ps[:, 6 + k % 2, 0:H + 1], probT[:, k % 2, P * j:P * j + P],
                                        rows[:, k, j, at_h:at_h + H + 1], start=(j == 0), stop=(j == 1))
                    ins.then_inc(s_summed, 1)
                keys = [(1, turn_keys)] if score is None else []
                over_units(pe, [(4, turn_probs)] + keys + [(2, scores), (4, sums)], walk)

            @block.scalar
            def _(act):
                def exps(u, k, rnd, b):
                    act.wait_ge(s_maxed, u + 1)
                    if reused(u, 2):
                        act.wait_ge(s_turnedp, u - 1)
                    act.activation(prob[:, k % 2, :], ps[:, 2 + k % 2, 0:UNIT], ACT.Exp, bias=ntop[:, k:k + 1]
                                   ).then_inc(s_prob, 1)
                    act.activation(shrink[:, k:k + 1], fall[:, k:k + 1], ACT.Exp).then_inc(s_shrunk, 1)

                def copy_keys(u, k, rnd, b):
                    act.wait_ge(s_turned, u + 1)
                    if reused(u, 2):
                        act.wait_ge(s_scored, u - 1)
                    act.copy(query[:, k % 2, :], queryT[0:H + 1, bass.ds(b * P, P)]).then_inc(s_query, 1)
                    act.copy(keyT[:, k % 2, :], ps[0:H + 1, k % 2, 0:UNIT]).then_inc(s_copied, 1)

                def bias(u, k, rnd, b):
                    act.wait_ge(s_outof, u + 1)
                    for j in range(2):
                        ins = act.activation(out_of[:, k % 4, j, :], out_of[:, k % 4, j, :], ACT.Identity,
                                             bias=rec[:, k, j, score:score + 1])
                    ins.then_inc(s_biased, 1)
                if score is None:
                    over_units(act, [(1, copy_keys), (3, exps)], walk, True)
                else:
                    over_units(act, [(3, exps), (1, bias)], walk)

            @block.vector
            def _(dve):
                def place_out(u, k, rnd, b):
                    dve.wait_ge(arrived[k], rnd * 16 + 16)
                    if reused(u, 4):
                        dve.wait_ge(s_scored, u - 3)
                    if score is None:
                        dve.wait_ge(gathered[k], rnd * 32 + 32)
                        dve.scalar_tensor_tensor(rows[:, k, :, 0:RBF], rec[:, k, :, 0:RBF], 0.1, rows[:, k, :, 0:RBF],
                                                 ALU.mult, ALU.add).then_inc(s_key, 1)
                    for j in range(2):
                        ins = dve.tensor_scalar(out_of[:, k % 4, j, :], c["iota"][:] if score is not None
                                                else c["iota16"][:], rec[:, k, j, place:place + 1], -BIG,
                                                ALU.not_equal, ALU.mult)
                    ins.then_inc(s_outof, 1)

                def tops(u, k, rnd, b):
                    dve.wait_ge(s_scored, u + 1)
                    dve.tensor_reduce(top[:, k:k + 1], ps[:, 2 + k % 2, 0:UNIT], AX, ALU.max).then_inc(s_linka, 1)

                def maxima(u, k, rnd, b):
                    nm = nmax[:, bass.ds(b, 1)]
                    dve.wait_ge(s_linka, u + 1)
                    if reused(u, 1):
                        dve.wait_ge(s_maxed, u)
                    dve.tensor_scalar(ntop[:, k:k + 1], top[:, k:k + 1], -1.0, nm, ALU.mult, ALU.min
                                      ).then_inc(s_linkb, 1)
                    dve.wait_ge(s_linkb, u * 2 + 1)
                    dve.tensor_tensor(fall[:, k:k + 1], ntop[:, k:k + 1], nm, ALU.subtract).then_inc(s_linkb, 1)
                    dve.wait_ge(s_linkb, u * 2 + 2)
                    dve.tensor_scalar(nm, ntop[:, k:k + 1], 0.0, None, ALU.add).then_inc(s_maxed, 1)

                def copy_probs(u, k, rnd, b):
                    dve.wait_ge(s_turnedp, u + 1)
                    if reused(u, 2):
                        dve.wait_ge(s_summed, u - 1)
                    dve.tensor_copy(probT[:, k % 2, :], ps[:, 4 + k % 2, 0:UNIT]).then_inc(s_copiedp, 1)

                def add(u, k, rnd, b):
                    dve.wait_ge(s_summed, u + 1)
                    dve.wait_ge(s_shrunk, u + 1)
                    if reused(u, 1):
                        dve.wait_ge(s_added, u)
                    a = acc[:, bass.ds(b, 1), :].rearrange("p o f -> p (o f)")
                    dve.scalar_tensor_tensor(a, a, shrink[:, k:k + 1], ps[:, 6 + k % 2, 0:H + 1], ALU.mult, ALU.add
                                             ).then_inc(s_added, 1)
                over_units(dve, [(3, tops), (4, copy_probs), (3, maxima), (5, add), (0, place_out)], walk, True)


def first_part(nc, c, m, ps, a, x, h, tmp, rec_dram, walk):
    table0 = nc.dram_tensor("table0", [NP, TAB0], F32).ap()
    table = nc.dram_tensor("table", [NP, TAB], F32).ap()
    rows_of = lambda t: t.rearrange("(b p) w -> p b w", p=P)
    mult, logm = m.sb("mult", [P, NB]), m.sb("logm", [P, NB])
    acc = m.sb("acc", [P, NB, H + 1])
    nmax = m.sb("nmax", [P, NB])
    tab = m.sb("tab", [P, NB, TAB])
    xT = m.sb("xT", [P, NP])
    vec = m.sb("vec", [P, 8, H])
    w = {"F1W": m.sb("F1W", [RBF, H]), "F1b": m.sb("F1b", [H, 1]), "F2": m.sb("F2", [H + 1, H]),
         "adapt": m.sb("adapt", [G, G])}
    everyone = lambda v: v.partition_broadcast(P)

    layer_norm(nc, "ln_in", x[:], h[:], tmp[:], relu=True)
    with ExitStack() as ctx:
        t = Memory(nc, ctx)
        z = t.sb("z", [P, NB], U32)
        embn = t.sb("embn", [P, NB, G])
        embp = t.sb("embp", [P, NB, 3 * G], BF16)
        rest = t.sb("embr", [P, NB, G])
        tab0 = t.sb("tab0", [P, NB, TAB0])
        send(nc, "load0", [(z[:].bitcast(I32), a["node_type"]),
                           (mult[:], a["node_vec"]),
                           (w["F1W"][:], a["F1W"]), (w["F1b"][:], a["F1b"].rearrange("(f o) -> f o", o=1)),
                           (w["F2"][0:H, :], a["F2W"]), (w["F2"][H:H + 1, :], a["F2b"].rearrange("(o f) -> o f", o=1)),
                           (w["adapt"][:], a["adapt"])])
        with stage(nc, "emb", "gathered", "step") as (block, gathered, step):
            @block.gpsimd
            def _(pool):
                for b in range(NB):
                    pool.indirect_dma_start(embn[:, b, :], None, a["emb"],
                                            bass.IndirectOffsetOnAxis(z[:, b:b + 1], 0)).then_inc(gathered, 16)
                pool.wait_ge(gathered, 16 * NB)

            @block.vector
            def _(dve):
                link = Link(dve, step)
                dve.memset(tab0[:, :, H + G:TAB0], 0.0)
                dve.memset(acc[:], 0.0)
                link(dve.tensor_copy(tab0[:, :, 0:H], h[:]))
                link(dve.tensor_copy(tab0[:, :, H + G], mult[:]))
                link(dve.tensor_scalar(logm[:], mult[:], 1.0, None, ALU.max))

            @block.scalar
            def _(act):
                act.wait_ge(step, 3)
                act.activation(logm[:], logm[:], ACT.Ln)
        with stage(nc, "embp", "step") as (block, step):
            @block.vector
            def _(dve):
                split(Link(dve, step), embn[:], rest[:], [embp[:, :, G * i:G * i + G] for i in range(3)])
        turn(nc, c, ps, "embT", embn[:], xT)
        times(nc, ps, "adapted", xT, w["adapt"][:], tab0[:, :, H:H + G])
        send(nc, "table0_out", [(rows_of(table0), tab0[:])])
        gate_edges(nc, c, ps, "gate", rec_dram, table0, embp, w, walk, acc)
    recip = m.sb("recip", [P, NB])

    def divide(link, floor, out):
        link(link.eng.tensor_scalar(recip[:], acc[:, :, H], floor, None, ALU.max))
        link(link.eng.reciprocal(recip[:], recip[:]))
        link(link.eng.tensor_tensor(out, acc[:, :, 0:H], bc(recip[:], H), ALU.mult))

    def plus(name, out, p, q):
        with stage(nc, name, "step") as (block, step):
            @block.vector
            def _(dve):
                dve.tensor_tensor(out, p, q, ALU.add)

    send(nc, "load1", [(vec[:, 0, :], everyone(a["gn"])), (vec[:, 1, :], everyone(a["bn"]))])
    with stage(nc, "mean0", "step") as (block, step):
        @block.vector
        def _(dve):
            link = Link(dve, step)
            divide(link, 1e-8, tmp[:])
            link(dve.tensor_tensor(h[:], h[:], tmp[:], ALU.add))
    layer_norm(nc, "ln0", h[:], h[:], tmp[:], gain=vec[:, 0, :], bias=vec[:, 1, :])

    wqk = m.sb("wqk", [H, 2 * H])
    wm, wmT, wub = m.sb("wm", [H, H]), m.sb("wmT", [H, H]), m.sb("wub", [H, H])
    wu = m.sb("wu", [64 + H, H])
    both = m.sb("both", [P, NB, 64 + H])[:]
    qk, q1 = both[:, :, 0:2 * H], m.sb("q1", [P, NB, H + 1])[:]
    queryT = m.sb("queryT", [H + 1, NP])
    with stage(nc, "wu_gap", "step") as (block, step):
        @block.vector
        def _(dve):
            dve.memset(wu[:], 0.0)
    with nc.Fori(0, LAYERS) as layer:
        at = lambda v: v[bass.ds(layer, 1)].rearrange("o k f -> (o k) f")
        row = lambda v: v[bass.ds(layer, 1), :].rearrange("o f -> (o f)").partition_broadcast(P)
        send(nc, "load_layer", [(wqk[:, 0:H], at(a["Wq"])), (wqk[:, H:2 * H], at(a["Wk"])), (wm[:], at(a["Wm"])),
                                (wu[0:H, :], a["Wu"][bass.ds(layer, 1), 0:H, :].rearrange("o k f -> (o k) f")),
                                (wub[:], a["Wu"][bass.ds(layer, 1), H:2 * H, :].rearrange("o k f -> (o k) f"))]
             + [(vec[:, n, :], row(a[v])) for n, v in enumerate(["gq", "bq", "gk", "bk", "go", "bo"])])
        with stage(nc, "weights", "turned", "copied", "summed") as (block, turned, copied, summed):
            @block.tensor
            def _(pe):
                pe.transpose(ps[0:H, 0, 0:H], wm[:], c["ident"][0:H, 0:H]).then_inc(turned, 1)
                pe.wait_ge(copied, 1)
                pe.matmul(ps[64:64 + H, 1, 0:H], wmT[:], wub[:], start=True, stop=True).then_inc(summed, 1)

            @block.vector
            def _(dve):
                dve.wait_ge(turned, 1)
                dve.tensor_copy(wmT[:], ps[0:H, 0, 0:H]).then_inc(copied, 1)
                dve.wait_ge(summed, 1)
                dve.tensor_copy(wu[64:64 + H, :], ps[64:64 + H, 1, 0:H])
        turn(nc, c, ps, "hT", h[:], xT)
        times(nc, ps, "qk", xT, wqk[:], qk)
        layer_norm(nc, "lnq", qk[:, :, 0:H], q1[:, :, 0:H], tmp[:], gain=vec[:, 0, :], bias=vec[:, 1, :])
        layer_norm(nc, "lnk", qk[:, :, H:2 * H], tab[:, :, 0:H], tmp[:], gain=vec[:, 2, :], bias=vec[:, 3, :])
        with stage(nc, "rows", "step") as (block, step):
            @block.vector
            def _(dve):
                dve.memset(q1[:, :, H:H + 1], 1.0)
                dve.tensor_copy(tab[:, :, H], logm[:])
                dve.tensor_copy(tab[:, :, H + 1:2 * H + 1], h[:])
                dve.memset(tab[:, :, 2 * H + 1:TAB], 1.0)
                dve.memset(acc[:], 0.0)
                dve.memset(nmax[:], NOMAX)
        turn(nc, c, ps, "qT", q1, queryT)
        send(nc, "table_out", [(rows_of(table), tab[:])])
        attend(nc, c, ps, "attend", rec_dram, REC, R_LOC, R_DST, None, table, TAB, H + 1, queryT, walk, acc, nmax)
        with stage(nc, "join", "step") as (block, step):
            @block.vector
            def _(dve):
                divide(Link(dve, step), 1e-10, both[:, :, 64:64 + H])
                dve.memset(both[:, :, H:64], 0.0)
                dve.tensor_copy(both[:, :, 0:H], h[:])
        turn(nc, c, ps, "bothT", both, xT)
        times(nc, ps, "update", xT, wu[:], tmp[:])
        with stage(nc, "leaky", "step") as (block, step):
            @block.vector
            def _(dve):
                link = Link(dve, step)
                link(dve.scalar_tensor_tensor(tmp[:], tmp[:], 0.01, tmp[:], ALU.mult, ALU.max))
                link(dve.tensor_tensor(h[:], h[:], tmp[:], ALU.add))
        layer_norm(nc, "lnh", h[:], h[:], tmp[:], gain=vec[:, 4, :], bias=vec[:, 5, :])
    plus("res1", x[:], x[:], h[:])



def second_part(nc, c, m, ps, x, h, tmp, rec_dram, walk):
    table = nc.dram_tensor("table1", [NP, TAB1], F32).ap()
    acc, nmax = m.sb("acc1", [P, NB, H + 1]), m.sb("nmax1", [P, NB])
    tab = m.sb("tab1", [P, NB, TAB1])
    recip = m.sb("recip1", [P, NB])
    layer_norm(nc, "ln1", x[:], h[:], tmp[:], relu=True)
    with stage(nc, "rows1", "step") as (block, step):
        @block.vector
        def _(dve):
            dve.tensor_copy(tab[:, :, 0:H], h[:])
            dve.memset(tab[:, :, H:TAB1], 1.0)
            dve.memset(acc[:], 0.0)
            dve.memset(nmax[:], NOMAX)
    send(nc, "table1_out", [(table.rearrange("(b p) w -> p b w", p=P), tab[:])])
    attend(nc, c, ps, "attend1", rec_dram, 4, R2_LOC, R2_SRC, R2_W1, table, TAB1, 0, None, walk, acc, nmax)
    with stage(nc, "elu", "step", "exp") as (block, step, s_exp):
        @block.vector
        def _(dve):
            link = Link(dve, step)
            link(dve.tensor_scalar(recip[:], acc[:, :, H], 1e-30, None, ALU.max))
            link(dve.reciprocal(recip[:], recip[:]))
            link(dve.tensor_tensor(h[:], acc[:, :, 0:H], bc(recip[:], H), ALU.mult))
            link(dve.tensor_scalar(tmp[:], h[:], 0.0, None, ALU.min))
            dve.wait_ge(s_exp, 1)
            link(dve.scalar_tensor_tensor(h[:], h[:], 0.0, tmp[:], ALU.max, ALU.add))
            link(dve.scalar_tensor_tensor(x[:], h[:], -1.0, x[:], ALU.add, ALU.add))

        @block.scalar
        def _(act):
            act.wait_ge(step, 4)
            act.activation(tmp[:], tmp[:], ACT.Exp).then_inc(s_exp, 1)



def count_edges(nc, m, ps, rec_dram, starts, C, spare, beside):
    BANKS = [(k * 512, min(512, NP - k * 512)) for k in range(-(-NP // 512))]
    ACT_BANKS = 4
    meta = spare[:, 0:4 * UNITS].rearrange("p (t w) -> p t w", w=2)
    ends = spare[:, 4 * UNITS:6 * UNITS]
    iota = m.sb("cnt_iota", [P, NP], I16)
    zero = m.sb("cnt_zero", [P, 512], BF16)
    wide = m.sb("cnt_wide", [P, 2, NP], BF16)
    hot = m.sb("cnt_hot", [P, 2, P], BF16)
    PIECES = 8
    with stage(nc, "count", "meta", "iota", "zero", "step", "made0", "made1", "used0", "used1", "full", "copied_a",
               "copied_v", *Scatter.SEMS) as (block, s_meta, s_iota, s_zero, s_step, made0, made1, used0, used1, s_full, s_copied_a,
                               s_copied_v, *others):
        made, used = (made0, made1), (used0, used1)

        def block_bounds(eng, b):
            read = lambda at: eng.value_load(starts[0:1, bass.ds(at, 1)], min_val=0, max_val=UNITS)
            return read(b), read(b + 1)

        @block.sync
        def _(sp):
            view = rec_dram[0:SLOTS, :].rearrange("(t p) w -> p t w", p=P)
            n = 2 * UNITS // PIECES
            for j in range(PIECES):
                sp.dma_start(meta[:, n * j:n * j + n, :], view[:, n * j:n * j + n, R_DST:R_LOC + 1]).then_inc(s_meta, 16)
            beside.load(sp, *others)

        @block.gpsimd
        def _(pool):
            pool.iota(iota[:], [[1, NP]], base=0, channel_multiplier=0).then_inc(s_iota, 1)
            beside.store(pool, *others)

        @block.vector
        def _(dve):
            dve.memset(zero[:], 0.0).then_inc(s_zero, 1)
            dve.sem_inc(s_copied_v, 1)
            dve.wait_ge(s_meta, 16 * PIECES)
            dve.tensor_copy(ends, meta[:, :, 0].bitcast(I32)).then_inc(s_step, 1)
            dve.wait_ge(s_step, 1)
            dve.wait_ge(s_iota, 1)
            with dve.Fori(0, NB) as b:
                first, end = block_bounds(dve, b)
                with dve.Fori(first, end) as u:
                    for j in range(2):
                        t = u * 2 + j
                        dve.wait_ge(used[j], u + 1)
                        dve.tensor_scalar(hot[:, j, :], iota[:, 0:P], meta[:, bass.ds(t, 1), 1], None, ALU.is_equal)
                        dve.tensor_scalar(wide[:, j, :], iota[:], ends[:, bass.ds(t, 1)], None, ALU.is_equal
                                          ).then_inc(made[j], 1)
                dve.wait_ge(s_full, b + 1)
                for n, (at, w) in enumerate(BANKS[ACT_BANKS:]):
                    ins = dve.tensor_copy(C[:, bass.ds(b, 1), at:at + w].rearrange("p o d -> p (o d)"),
                                          ps[:, ACT_BANKS + n, 0:w])
                ins.then_inc(s_copied_v, 1)

        @block.tensor
        def _(pe):
            for j in range(2):
                pe.sem_inc(used[j], 1)
            pe.wait_ge(s_zero, 1)
            with pe.Fori(0, NB) as b:
                first, end = block_bounds(pe, b)
                pe.wait_ge(s_copied_a, b + 1)
                pe.wait_ge(s_copied_v, b + 1)
                for n, (at, w) in enumerate(BANKS):
                    pe.matmul(ps[:, n, 0:w], zero[:, 0:P], zero[:, 0:w], start=True, stop=False)
                with pe.Fori(first, end) as u:
                    for j in range(2):
                        pe.wait_ge(made[j], u + 1)
                        for n, (at, w) in enumerate(BANKS):
                            ins = pe.matmul(ps[:, n, 0:w], hot[:, j, :], wide[:, j, at:at + w], start=False, stop=False)
                        ins.then_inc(used[j], 1)
                for n, (at, w) in enumerate(BANKS):
                    ins = pe.matmul(ps[:, n, 0:w], zero[:, 0:P], zero[:, 0:w], start=False, stop=True)
                ins.then_inc(s_full, 1)

        @block.scalar
        def _(act):
            act.sem_inc(s_copied_a, 1)
            with act.Fori(0, NB) as b:
                act.wait_ge(s_full, b + 1)
                for n, (at, w) in enumerate(BANKS[:ACT_BANKS]):
                    ins = act.copy(C[:, bass.ds(b, 1), at:at + w].rearrange("p o d -> p (o d)"), ps[:, n, 0:w])
                ins.then_inc(s_copied_a, 1)


def degrees(nc, c, m, ps, C, dinv, many, rec_dram, walk, spare):
    HALF = (NB + 1) // 2
    top, big = m.sb("deg_top", [P, 1]), m.sb("deg_big", [P, 1])
    squares = m.sb("deg_squares", [P, NB - HALF])
    junk = spare[:, 0:NP // 2].bitcast(BF16)
    with stage(nc, "degrees", "summed", "top", "turned", "step", "squared") as (
            block, s_summed, s_top, s_turned, step, s_squared):
        @block.scalar
        def _(act):
            for n in range(NB - HALF):
                if n:
                    act.wait_ge(s_squared, n)
                act.activation(junk, C[:, HALF + n, :], ACT.Square, accum_out=squares[:, n:n + 1]
                               ).then_inc(s_squared, 1)

        @block.tensor
        def _(pe):
            for d in range(NB):
                for s in range(NB):
                    ins = pe.matmul(ps[:, 0, d:d + 1], C[:, s, P * d:P * d + P], c["onesb"][:, 0:1],
                                    start=(s == 0), stop=(s == NB - 1))
            ins.then_inc(s_summed, 1)
            pe.wait_ge(s_top, 1)
            pe.transpose(ps[0:1, 1, 0:P], top[:], c["ident"][:]).then_inc(s_turned, 1)

        @block.vector
        def _(dve):
            link = Link(dve, step)
            link(dve.tensor_reduce(top[:], C[:, 0:HALF].rearrange("p b d -> p (b d)"), AX, ALU.max))
            dve.wait_ge(s_squared, NB - HALF)
            link(dve.tensor_reduce(big[:], squares[:], AX, ALU.max))
            link(dve.tensor_scalar(big[:], big[:], float(256 ** 2), 256.0, ALU.is_ge, ALU.mult))
            dve.tensor_tensor(top[:], top[:], big[:], ALU.max).then_inc(s_top, 1)
            dve.wait_ge(s_summed, 1)
            link(dve.tensor_scalar(dinv[:], ps[:, 0, 0:NB], 1.0, None, ALU.add))
            dve.wait_ge(s_turned, 1)
            link(dve.tensor_reduce(top[0:1, :], ps[0:1, 1, 0:P], AX, ALU.max))
            link(dve.tensor_scalar(top[0:1, :], top[0:1, :], 256.0, None, ALU.is_ge))
            link(dve.tensor_copy(many[0:1, :], top[0:1, :]))
    with ExitStack() as ctx:
        recount_degrees(nc, c, Memory(nc, ctx), ps, dinv, many, rec_dram, walk)
    with stage(nc, "dinv", "root") as (block, s_root):
        @block.scalar
        def _(act):
            act.sqrt(dinv[:], dinv[:]).then_inc(s_root, 1)

        @block.vector
        def _(dve):
            dve.wait_ge(s_root, 1)
            dve.reciprocal(dinv[:], dinv[:])


def needed(eng, many):
    return eng.If(eng.value_load(many[0:1, 0:1], min_val=0, max_val=1) > 0)


def recount_degrees(nc, c, m, ps, deg, many, rec_dram, walk):
    rec = m.sb("deg_rec", [P, RING, 2, 4])
    hot = m.sb("deg_hot", [P, 2, 2, P])
    with stage(nc, "deg_again", "clear", "hot", "summed", "added", *[f"rec{k}" for k in range(RING)]) as (
            block, s_clear, s_hot, s_summed, s_added, *arrived):
        @block.sync
        def _(sp):
            with needed(sp, many):
                load_records(rec, rec_dram, arrived, [s_hot], walk)(sp)

        @block.vector
        def _(dve):
            def one_hot(u, k, rnd, b):
                dve.wait_ge(arrived[k], rnd * 16 + 16)
                if reused(u, 2):
                    dve.wait_ge(s_summed, u - 1)
                for j in range(2):
                    ins = dve.tensor_scalar(hot[:, k % 2, j, :], c["iota"][:], rec[:, k, j, R2_LOC:R2_LOC + 1], None,
                                            ALU.is_equal)
                ins.then_inc(s_hot, 1)

            def add(u, k, rnd, b):
                dve.wait_ge(s_summed, u + 1)
                if reused(u, 1):
                    dve.wait_ge(s_added, u)
                o = deg[:, bass.ds(b, 1)]
                dve.tensor_tensor(o, o, ps[:, k % 2, 0:1], ALU.add).then_inc(s_added, 1)
            with needed(dve, many):
                dve.tensor_scalar(deg[:], deg[:], 0.0, 1.0, ALU.mult, ALU.add).then_inc(s_clear, 1)
                dve.wait_ge(s_clear, 1)
                over_units(dve, [(0, one_hot), (1, add)], walk, True)

        @block.tensor
        def _(pe):
            def sums(u, k, rnd, b):
                pe.wait_ge(s_hot, u + 1)
                if reused(u, 2):
                    pe.wait_ge(s_added, u - 1)
                for j in range(2):
                    ins = pe.matmul(ps[:, k % 2, 0:H], hot[:, k % 2, j, :], c["ones"][:, 0:H], start=(j == 0),
                                    stop=(j == 1))
                ins.then_inc(s_summed, 1)
            with needed(pe, many):
                over_units(pe, [(0, sums)], walk)


class Spread:

    def __init__(self, nc, c, ps, C, dinv, many, rec_dram, walk):
        self.nc, self.c, self.ps, self.C, self.dinv, self.many = nc, c, ps, C, dinv, many
        self.rec_dram, self.walk = rec_dram, walk
        self.table = nc.dram_tensor("table2", [NP, H], F32).ap()

    def finish(self, link, out, start):
        dve = link.eng
        link(dve.tensor_tensor(out, out, self.scaled[:], ALU.add))
        link(dve.tensor_tensor(out, out, bc(self.dinv[:], H), ALU.mult))
        if start is not None:
            link(dve.scalar_tensor_tensor(out, out, 0.2, start, ALU.mult, ALU.add))

    def __call__(self, name, g, out, start=None):
        with ExitStack() as ctx:
            m = Memory(self.nc, ctx)
            self.parts = m.sb(f"{name}_parts", [P, NB, 3, H], BF16)
            self.scaled = m.sb(f"{name}_scaled", [P, NB, H])
            self.run(name, g, out, start)

    def run(self, name, g, out, start):
        nc, ps, C, parts, scaled, dinv = self.nc, self.ps, self.C, self.parts, self.scaled, self.dinv
        D = 5
        with stage(nc, name, "split", "step", "summed", "added") as (block, s_split, step, s_summed, s_added):
            @block.vector
            def _(dve):
                link = Link(dve, step)
                link(dve.tensor_tensor(scaled[:], g, bc(dinv[:], H), ALU.mult))
                split(link, scaled[:], out, [parts[:, :, i, :] for i in range(3)])
                dve.sem_inc(s_split, 1)
                dve.sem_inc(s_added, 1)
                with dve.Fori(0, NB // D) as i:
                    for j in range(D):
                        dve.wait_ge(s_summed, i * D + (j + 1))
                        o = out[:, bass.ds(i * D + j, 1), :].rearrange("p o f -> p (o f)")
                        dve.tensor_reduce(o, ps[:, j, 0:3 * H].rearrange("p (k f) -> p f k", f=H), AX, ALU.add
                                          ).then_inc(s_added, 1)
                dve.wait_ge(s_added, NB + 1)
                self.finish(link, out, start)

            @block.tensor
            def _(pe):
                pe.wait_ge(s_split, 1)
                with pe.Fori(0, NB // D) as i:
                    for j in range(D):
                        pe.wait_ge(s_added, i * D + 1)
                        for s in range(NB):
                            ins = pe.matmul(ps[:, j, 0:3 * H], C[:, s, bass.ds(i * (D * P) + j * P, P)],
                                            parts[:, s].rearrange("p k f -> p (k f)"),
                                            start=(s == 0), stop=(s == NB - 1))
                        ins.then_inc(s_summed, 1)
        self.recount(name + "_again", out, start)

    def recount(self, name, out, start):
        nc, ps, c = self.nc, self.ps, self.c
        words = self.parts[:].rearrange("p b k f -> p (b k f)").bitcast(F32)
        n = 2 * RING
        rec = words[:, 0:4 * n].rearrange("p (k j w) -> p k j w", j=2, w=4)
        rows = words[:, 4 * n:(4 + H) * n].rearrange("p (k j w) -> p k j w", j=2, w=H)
        hot = words[:, (4 + H) * n:(4 + H) * n + 4 * P].rearrange("p (k j w) -> p k j w", j=2, w=P)
        with stage(nc, name, "table", "clear", "hot", "summed", "added", "passed", "step",
                   *[f"rec{k}" for k in range(RING)], *[f"row{k}" for k in range(RING)]) as (
                block, s_table, s_clear, s_hot, s_summed, s_added, s_passed, step, *dmas):
            arrived, gathered = dmas[:RING], dmas[RING:]

            @block.sync
            def _(sp):
                with needed(sp, self.many):
                    sp.dma_start(self.table.rearrange("(b p) w -> p b w", p=P), self.scaled[:]).then_inc(s_table, 16)
                    load_records(rec, self.rec_dram, arrived, [s_hot, s_summed], self.walk)(sp)

            @block.gpsimd
            def _(pool):
                with needed(pool, self.many):
                    pool.wait_ge(s_table, 16)
                    gather_rows(rec, R2_SRC, self.table, rows, arrived, gathered, s_summed, s_passed,
                                self.walk)(pool)

            @block.vector
            def _(dve):
                def one_hot(u, k, rnd, b):
                    dve.wait_ge(arrived[k], rnd * 16 + 16)
                    if reused(u, 2):
                        dve.wait_ge(s_summed, u - 1)
                    for j in range(2):
                        ins = dve.tensor_scalar(hot[:, k % 2, j, :], c["iota"][:], rec[:, k, j, R2_LOC:R2_LOC + 1],
                                                None, ALU.is_equal)
                    ins.then_inc(s_hot, 1)

                def add(u, k, rnd, b):
                    dve.wait_ge(s_summed, u + 1)
                    if reused(u, 1):
                        dve.wait_ge(s_added, u)
                    o = out[:, bass.ds(b, 1), :].rearrange("p o f -> p (o f)")
                    dve.tensor_tensor(o, o, ps[:, k % 2, 0:H], ALU.add).then_inc(s_added, 1)
                with needed(dve, self.many):
                    dve.tensor_scalar(out, out, 0.0, None, ALU.mult).then_inc(s_clear, 1)
                    dve.wait_ge(s_clear, 1)
                    over_units(dve, [(0, one_hot), (1, add)], self.walk, True)
                    dve.wait_ge(s_added, bodies_of(dve, self.walk) * RING)
                    self.finish(Link(dve, step), out, start)

            @block.tensor
            def _(pe):
                def sums(u, k, rnd, b):
                    pe.wait_ge(s_hot, u + 1)
                    pe.wait_ge(gathered[k], rnd * 32 + 32)
                    if reused(u, 2):
                        pe.wait_ge(s_added, u - 1)
                    for j in range(2):
                        ins = pe.matmul(ps[:, k % 2, 0:H], hot[:, k % 2, j, :], rows[:, k, j, :],
                                        start=(j == 0), stop=(j == 1))
                    ins.then_inc(s_summed, 1)
                with needed(pe, self.many):
                    over_units(pe, [(0, sums)], self.walk)



def third_part(nc, m, x, h, tmp, spread):
    with ExitStack() as ctx:
        t = Memory(nc, ctx)
        start = t.sb("start", [P, NB, H])
        layer_norm(nc, "ln2", x[:], h[:], tmp[:], relu=True)
        with stage(nc, "start", "step") as (block, step):
            @block.vector
            def _(dve):
                dve.tensor_scalar(start[:], h[:], 0.8, None, ALU.mult)
        with nc.Fori(0, 5):
            spread("step", h[:], h[:], start[:])
        with stage(nc, "res2", "step") as (block, step):
            @block.vector
            def _(dve):
                dve.tensor_tensor(x[:], x[:], h[:], ALU.add)



def batch_norm(nc, c, ps, name, y, sq, gain, bias, before, relu_before=False, relu_after=False, eps=1e-5):
    with ExitStack() as ctx:
        m = Memory(nc, ctx)
        mean, var, part = (m.sb(f"{name}_{k}", [P, H]) for k in ("mean", "var", "part"))
        with stage(nc, name, "step", "ready", "summed", "root") as (block, step, s_ready, s_summed, s_root):
            @block.tensor
            def _(pe):
                for n, v in enumerate((y, sq)):
                    pe.wait_ge(s_ready, n + 1)
                    pe.matmul(ps[:, n, 0:H], c["ones"][:], part[:], start=True, stop=False)
                    pe.matmul(ps[:, n, 0:H], c["some"][:], v[:, NB - 1, :], start=False, stop=True).then_inc(s_summed, 1)

            @block.vector
            def _(dve):
                link = Link(dve, step)
                over_blocks = lambda v: v[:, 0:NB - 1, :].rearrange("p b f -> p f b")
                link(dve.tensor_tensor(y, y, along(before, NB), ALU.add))
                if relu_before:
                    link(dve.tensor_scalar(y, y, 0.0, None, ALU.max))
                dve.tensor_reduce(part[:], over_blocks(y), AX, ALU.add).then_inc(s_ready, 1)
                dve.wait_ge(s_summed, 1)
                link(dve.tensor_scalar(mean[:], ps[:, 0, 0:H], 1.0 / N, None, ALU.mult))
                link(dve.tensor_tensor(y, y, along(mean[:], NB), ALU.subtract))
                link(dve.tensor_tensor(sq, y, y, ALU.mult))
                dve.tensor_reduce(part[:], over_blocks(sq), AX, ALU.add).then_inc(s_ready, 1)
                dve.wait_ge(s_summed, 2)
                link(dve.tensor_scalar(var[:], ps[:, 1, 0:H], 1.0 / N, eps, ALU.mult, ALU.add))
                dve.wait_ge(s_root, 1)
                link(dve.reciprocal(var[:], var[:]))
                link(dve.tensor_tensor(var[:], var[:], gain, ALU.mult))
                link(dve.tensor_tensor(y, y, along(var[:], NB), ALU.mult))
                link(dve.tensor_tensor(y, y, along(bias, NB), ALU.add))
                if relu_after:
                    link(dve.tensor_scalar(y, y, 0.0, None, ALU.max))

            @block.scalar
            def _(act):
                act.wait_ge(step, 5 + relu_before)
                act.sqrt(var[:], var[:]).then_inc(s_root, 1)


def hidden(nc, c, m, ps, y, memory, z, w1, w2, cols, spare, eps=1e-5):
    PER = 2
    groups = [range(b, min(b + PER, NB)) for b in range(0, NB, PER)]
    sums = [range(b, min(b + 3, NB)) for b in range(0, NB, 3)]
    pieces = [(at, min(512, N - at)) for at in range(0, N, 512)]
    xT = spare[0:FC, 0:4 * PER * P].rearrange("p (h i n) -> p h i n", h=2, i=2)
    mean, var = m.sb("hid_mean", [MC, 1]), m.sb("hid_var", [MC, 1])
    squares = m.sb("hid_squares", [MC, len(pieces)])
    hT, junk = memory[:, 0:NP], memory[:, NP:NP + 256].bitcast(BF16)
    with stage(nc, "hidden", "turned", "copied", "mixed", "relu", "step", "squared", "root", "normed", "summed",
               "added") as (block, s_turned, s_copied, s_mixed, s_relu, step, s_squared, s_root, s_normed, s_summed,
                            s_added):
        @block.tensor
        def _(pe):
            def turn_in(g):
                if g >= 2:
                    pe.wait_ge(s_copied, (g - 1) * 2)
                for i in range(2):
                    for j, b in enumerate(groups[g]):
                        ins = pe.transpose(ps[0:FC, 2 * (g % 2) + i, P * j:P * j + P], y[:, b, FC * i:FC * i + FC],
                                           c["ident"][:])
                    ins.then_inc(s_turned, 1)

            def mix(g):
                pe.wait_ge(s_copied, (g + 1) * 2)
                if g >= 2:
                    pe.wait_ge(s_relu, g - 1)
                n = len(groups[g]) * P
                for i in range(2):
                    ins = pe.matmul(ps[0:MC, 4 + g % 2, 0:n], w1[:, i, :], xT[:, g % 2, i, 0:n], start=(i == 0),
                                    stop=(i == 1))
                ins.then_inc(s_mixed, 1)
            for g in range(len(groups) + 1):
                if g < len(groups):
                    turn_in(g)
                if g:
                    mix(g - 1)
            pe.wait_ge(s_normed, 1)
            for q, bs in enumerate(sums):
                if q >= 2:
                    pe.wait_ge(s_added, q - 1)
                for j, b in enumerate(bs):
                    ins = pe.matmul(ps[:, 6 + q % 2, C3 * j:C3 * j + C3], hT[:, P * b:P * b + P], w2, start=True,
                                    stop=True)
                ins.then_inc(s_summed, 1)

        @block.scalar
        def _(act):
            def copy_in(g):
                n = len(groups[g]) * P
                if g >= 2:
                    act.wait_ge(s_mixed, g - 1)
                for i in range(2):
                    act.wait_ge(s_turned, g * 2 + i + 1)
                    act.copy(xT[:, g % 2, i, 0:n], ps[0:FC, 2 * (g % 2) + i, 0:n]).then_inc(s_copied, 1)

            def relu(g):
                n = len(groups[g]) * P
                act.wait_ge(s_mixed, g + 1)
                act.activation(hT[:, g * PER * P:g * PER * P + n], ps[0:MC, 4 + g % 2, 0:n], ACT.Relu,
                               bias=cols[:, 0:1]).then_inc(s_relu, 1)
            for g in range(len(groups) + 1):
                if g < len(groups):
                    copy_in(g)
                if g:
                    relu(g - 1)
            act.wait_ge(step, 3)
            for n, (at, width) in enumerate(pieces):
                if n:
                    act.wait_ge(s_squared, n)
                act.activation(junk[:, 0:width], hT[:, at:at + width], ACT.Square, accum_out=squares[:, n:n + 1]
                               ).then_inc(s_squared, 1)
            act.wait_ge(step, 5)
            act.sqrt(var[:], var[:]).then_inc(s_root, 1)

        @block.vector
        def _(dve):
            link = Link(dve, step)
            dve.wait_ge(s_relu, len(groups))
            link(dve.tensor_reduce(mean[:], hT[:, 0:N], AX, ALU.add))
            link(dve.tensor_scalar(mean[:], mean[:], -1.0 / N, None, ALU.mult))
            link(dve.tensor_scalar(hT, hT, mean[:], None, ALU.add))
            dve.wait_ge(s_squared, len(pieces))
            link(dve.tensor_reduce(var[:], squares[:], AX, ALU.add))
            link(dve.tensor_scalar(var[:], var[:], 1.0 / N, eps, ALU.mult, ALU.add))
            dve.wait_ge(s_root, 1)
            link(dve.reciprocal(var[:], var[:]))
            link(dve.tensor_tensor(var[:], var[:], cols[:, 1:2], ALU.mult))
            dve.tensor_scalar(hT, hT, var[:], cols[:, 2:3], ALU.mult, ALU.add).then_inc(s_normed, 1)
            for q, bs in enumerate(sums):
                dve.wait_ge(s_summed, q + 1)
                o = z[:, bs[0]:bs[-1] + 1, :]
                dve.tensor_tensor(o, o, ps[:, 6 + q % 2, 0:C3 * len(bs)].rearrange("p (b f) -> p b f", f=C3), ALU.add
                                  ).then_inc(s_added, 1)


def stream(nc, c, ps, name, x, w, out, spare):
    K, k, f = w.shape
    per = 3 if k == 1 else 2
    groups = [range(b, min(b + per, NB)) for b in range(0, NB, per)]
    xT = spare[0:K, 0:2 * k * per * P].rearrange("p (h i n) -> p h i n", h=2, i=k)
    with stage(nc, name, "turned", "copied", "summed", "out") as (block, s_turned, s_copied, s_summed, s_out):
        @block.tensor
        def _(pe):
            def turn_in(g):
                if g >= 2:
                    pe.wait_ge(s_copied, (g - 1) * k)
                for i in range(k):
                    for j, b in enumerate(groups[g]):
                        ins = pe.transpose(ps[0:K, 2 * (g % 2) + i, P * j:P * j + P], x[:, b, K * i:K * i + K],
                                           c["ident"][:])
                    ins.then_inc(s_turned, 1)

            def products(g):
                pe.wait_ge(s_copied, (g + 1) * k)
                if g >= 2:
                    pe.wait_ge(s_out, g - 1)
                for j, b in enumerate(groups[g]):
                    for i in range(k):
                        ins = pe.matmul(ps[:, 4 + g % 2, f * j:f * j + f], xT[:, g % 2, i, P * j:P * j + P],
                                        w[:, i, :], start=(i == 0), stop=(i == k - 1))
                ins.then_inc(s_summed, 1)
            for g in range(len(groups) + 1):
                if g < len(groups):
                    turn_in(g)
                if g:
                    products(g - 1)

        @block.scalar
        def _(act):
            for g, bs in enumerate(groups):
                n = len(bs) * P
                if g >= 2:
                    act.wait_ge(s_summed, g - 1)
                for i in range(k):
                    act.wait_ge(s_turned, g * k + i + 1)
                    act.copy(xT[:, g % 2, i, 0:n], ps[0:K, 2 * (g % 2) + i, 0:n]).then_inc(s_copied, 1)

        @block.vector
        def _(dve):
            for g, bs in enumerate(groups):
                dve.wait_ge(s_summed, g + 1)
                o = out[:, bs[0]:bs[-1] + 1, :]
                p = ps[:, 4 + g % 2, 0:f * len(bs)].rearrange("p (b f) -> p b f", f=f)
                dve.tensor_copy(o, p).then_inc(s_out, 1)


def fourth_part(nc, c, m, ps, a, x, h, tmp, wide, spread):
    kept = nc.dram_tensor("kept", [P, NB, H], F32).ap()
    te = nc.dram_tensor("time_rows", [1, C9 + C3], F32).ap()
    spare = x[:].rearrange("p b f -> p (b f)")
    wc1 = m.sb("wc1", [FC, 2, MC])
    wc2 = spare[0:MC, 1024:1024 + C3]
    cols = m.sb("cols_now", [MC, 3])
    behind = wide[:, 2 * NB * H:3 * NB * H]
    rows = behind[:, 0:3 * H].rearrange("p (k f) -> p k f", k=3)
    w_in = behind[0:H, 3 * H:3 * H + C3].rearrange("p (k f) -> p k f", k=1)
    w_out = behind[0:FC, 3 * H:5 * H].rearrange("p (k f) -> p k f", k=2)
    columns = lambda v, j: v[:, :, bass.ds(j * H, H)]
    part = lambda v, j: v[bass.ds(j * H, H)].partition_broadcast(P)
    halves = lambda sb, dram: [(sb[:, i, :], dram[FC * i:FC * i + FC]) for i in range(2)]

    def norm(name, j, y, sq, names, more=(), **relus):
        send(nc, name + "_rows", [(rows[:, n, :], part(v, j)) for n, v in enumerate(names)] + list(more))
        batch_norm(nc, c, ps, name, y, sq, rows[:, 1, :], rows[:, 2, :], before=rows[:, 0, :], **relus)

    def move(name, to, what):
        with stage(nc, name) as (block,):
            @block.vector
            def _(dve):
                dve.tensor_copy(to, what)

    time_rows(nc, ps, a, te)
    te1, te2 = te[0, 0:C9], te[0, C9:]
    layer_norm(nc, "ln3", x[:], h[:], tmp[:], relu=True)
    send(nc, "load3", [(kept, x[:]), (w_in[:, 0, :], a["W_in"])])
    y = m.sb("wide", [P, NB, C3])
    spread("conv_in", h[:], tmp[:])
    stream(nc, c, ps, "in_w", tmp[:], w_in[:], y[:], spare)
    with nc.Fori(0, C3 // H) as j:
        norm("bn_in", j, columns(y[:], j), tmp[:], [a["b_in"], a["g_in"], a["be_in"]], relu_after=True)
        spread("conv1", columns(y[:], j), columns(y[:], j))
    with ExitStack() as ctx:
        z = Memory(nc, ctx).sb("mixed", [P, NB, C3])
        with stage(nc, "clear_z") as (block,):
            @block.vector
            def _(dve):
                dve.memset(z[:], 0.0)
        with nc.Fori(0, C9 // MC) as j:
            now = bass.ds(j * MC, MC)
            send(nc, "load_c", [(wc1[:, i, :], a["Wc1"][FC * i:FC * i + FC, now]) for i in range(2)]
                 + [(wc2[:], a["Wc2"][now, :])]
                 + [(cols[:, n:n + 1], v[now].rearrange("(p o) -> p o", o=1))
                    for n, v in enumerate([te1, a["g1"], a["be1"]])])
            with ExitStack() as ctx2:
                hidden(nc, c, Memory(nc, ctx2), ps, y, wide[0:MC, :], z, wc1, wc2[:], cols, spare)
        move("keep_z", y[:], z[:])
    with nc.Fori(0, C3 // H) as j:
        spread("conv2", columns(y[:], j), columns(y[:], j))
        norm("bn2", j, columns(y[:], j), tmp[:], [te2, a["g2"], a["be2"]], relu_before=True)
    send(nc, "load_out", halves(w_out, a["W_out"]))
    stream(nc, c, ps, "out_w", y[:], w_out[:], h[:], spare)
    spread("conv_out", h[:], tmp[:])
    norm("bn_out", 0, tmp[:], h[:], [a["b_out"], a["g_out"], a["be_out"]], more=[(x[:], kept)], relu_after=True)
    with stage(nc, "res3") as (block,):
        @block.vector
        def _(dve):
            dve.tensor_tensor(x[:], x[:], tmp[:], ALU.add)


def time_rows(nc, ps, a, te):
    with ExitStack() as ctx:
        m = Memory(nc, ctx)
        ang, turns, k, freq = (m.sb(f"time_{n}", [T, 1]) for n in ("ang", "turns", "k", "freq"))
        bias = m.sb("time_bias", [T, 1])
        wtm, wt = m.sb("time_wtm", [T, T]), m.sb("time_wt", [T, C9 + C3])
        bt, cb = m.sb("time_bt", [1, C9 + C3]), m.sb("time_cb", [1, C9 + C3])
        flat = lambda v: v.rearrange("(o f) -> o f", o=1)
        send(nc, "load_time", [(ang[:], a["timestep"].partition_broadcast(T)), (freq[:], a["freqs"]), (wtm[:], a["Wtm"]),
                               (wt[:, 0:C9], a["Wt1"]), (wt[:, C9:], a["Wt2"]),
                               (bias[:], a["btm"].rearrange("(p o) -> p o", o=1)),
                               (bt[:, 0:C9], flat(a["bt1"])), (bt[:, C9:], flat(a["bt2"])),
                               (cb[:, 0:C9], flat(a["bc1"])), (cb[:, C9:], flat(a["bc2"]))])
        with stage(nc, "time", "step", "sin", "mixed", "relu", "rows") as (block, step, s_sin, s_mixed, s_relu, s_rows):
            R = 12582912.0
            PI2 = (6.28125, float(np.float32(2 * math.pi - 6.28125)),
                   2 * math.pi - 6.28125 - float(np.float32(2 * math.pi - 6.28125)))

            @block.vector
            def _(dve):
                link = Link(dve, step)
                link(dve.tensor_tensor(ang[:], ang[:], freq[:], ALU.mult))
                link(dve.tensor_scalar(turns[:], ang[:], 0.5 / math.pi, None, ALU.mult))
                link(dve.tensor_scalar(turns[T // 2:, :], turns[T // 2:, :], 0.25, None, ALU.add))
                link(dve.tensor_scalar(k[:], turns[:], R, None, ALU.add))
                link(dve.tensor_scalar(k[:], k[:], -R, None, ALU.add))
                for part in PI2:
                    link(dve.scalar_tensor_tensor(ang[:], k[:], -part, ang[:], ALU.mult, ALU.add))
                link(dve.tensor_scalar(ang[T // 2:, :], ang[T // 2:, :], math.pi / 2, None, ALU.add))
                link(dve.tensor_scalar(ang[:], ang[:], 3.1415925, -3.1415925, ALU.min, ALU.max))
                dve.wait_ge(s_mixed, 1)
                link(dve.scalar_tensor_tensor(ang[:], ps[0:T, 0, 0:1], 1.0, bias[:], ALU.mult, ALU.add))
                dve.tensor_scalar(ang[:], ang[:], 0.0, None, ALU.max).then_inc(s_relu, 1)
                dve.wait_ge(s_rows, 1)
                link(dve.tensor_tensor(bt[:, 0:C9], bt[:, 0:C9], ps[0:1, 1, 0:C9], ALU.add))
                link(dve.tensor_tensor(bt[:, C9:], bt[:, C9:], ps[0:1, 2, 0:C3], ALU.add))
                link(dve.scalar_tensor_tensor(bt[:], bt[:], 0.0, cb[:], ALU.max, ALU.add))

            @block.scalar
            def _(act):
                act.wait_ge(step, 10)
                act.activation(turns[:], ang[:], ACT.Sin).then_inc(s_sin, 1)

            @block.tensor
            def _(pe):
                pe.wait_ge(s_sin, 1)
                pe.matmul(ps[0:T, 0, 0:1], wtm[:], turns[:], start=True, stop=True).then_inc(s_mixed, 1)
                pe.wait_ge(s_relu, 1)
                pe.matmul(ps[0:1, 1, 0:C9], ang[:], wt[:, 0:C9], start=True, stop=True)
                pe.matmul(ps[0:1, 2, 0:C3], ang[:], wt[:, C9:], start=True, stop=True).then_inc(s_rows, 1)
        send(nc, "time_out", [(te, bt[:])])


def cutoff_words(nc, m, a, meta, word, loc):
    cut, far, end = word[0], word[1], word[2].bitcast(I32)
    half_pi = m.sb("half_pi", [P, 1])
    with stage(nc, "cutoff", "in", "step", "cos") as (block, s_in, step, cos):
        @block.sync
        def _(sp):
            sp.dma_start(cut, a["ew"]).then_inc(s_in, 16)
            sp.dma_start(end, a["dst"]).then_inc(s_in, 16)

        @block.vector
        def _(dve):
            link = Link(dve, step)
            dve.memset(half_pi[:], math.pi / 2)
            dve.memset(meta[:, :, 0:2], 0.0)
            dve.tensor_copy(meta[:, :, 3], loc[:])
            dve.wait_ge(s_in, 32)
            dve.tensor_copy(meta[:, :, 2].bitcast(I32), end)
            link(dve.tensor_scalar(far, cut, 6.0, None, ALU.is_lt))
            link(dve.tensor_scalar(cut, cut, 6.0, -6.0, ALU.min, ALU.max))
            link(dve.scalar_tensor_tensor(cut, cut, -1.0, cut, ALU.mult, ALU.max))
            dve.wait_ge(cos, 1)
            link(dve.tensor_scalar(cut, cut, 1.0, 0.5, ALU.add, ALU.mult))
            link(dve.tensor_tensor(meta[:, :, 0], cut, far, ALU.mult))

        @block.scalar
        def _(act):
            act.wait_ge(step, 3)
            act.activation(cut, cut, ACT.Sin, bias=half_pi[:], scale=-math.pi / 6).then_inc(cos, 1)


def network(nc, m, ps, a, o):
    filled = nc.alloc_semaphore("filled")
    out_done = nc.alloc_semaphore("out_done")
    rec1 = nc.dram_tensor("edges_by_src", [SLOTS + P * (TW - TILES + 1), REC], F32).ap()
    rec2 = nc.dram_tensor("edges_by_dst", [SLOTS + P * (TW - TILES + 1), 4], F32).ap()
    blocks1, blocks2 = m.sb("blocks1", [P, BODIES + 1], I32), m.sb("blocks2", [P, BODIES + 1], I32)
    starts1, starts2 = m.sb("starts1", [P, NB + 2], I32), m.sb("starts2", [P, NB + 2], I32)
    walk1, walk2 = ((w[:], s[0:1, NB + 1:NB + 2]) for w, s in ((blocks1, starts1), (blocks2, starts2)))
    x = m.sb("nodes_x", [P, NB, H])
    nodes = m.sb("nodes", [P, 3, NB, H])
    h, tmp = nodes[:, 0], nodes[:, 1]
    flat_nodes = nodes[:].rearrange("p k b f -> p (k b f)")
    c = constants(nc, m, flat_nodes[:, 0:P // 2].bitcast(BF16))

    meta1, meta2 = (nc.dram_tensor(f"meta{n}", [P, TW, 4], F32).ap() for n in (1, 2))
    pos1, pos2 = (nc.dram_tensor(f"pos{n}", [P, TW], U32).ap() for n in (1, 2))
    with ExitStack() as ctx:
        t = Memory(nc, ctx)
        big = t.sb("big", [P, 2 * TW * NB + NB])
        n_filled = prefill(nc, flat_nodes[:, P // 2:], [(rec1, REC, R_LOC), (rec2, 4, R2_LOC)], filled)
        pos = t.sb("pos", [P, TW], U32)
        loc = t.sb("loc", [P, TW])
        meta = big[:, 0:4 * TW].rearrange("p (t w) -> p t w", w=4)
        word = [big[:, n * TW:(n + 1) * TW] for n in range(4, 8)]
        group(nc, c, ps, "by_src", a["src"], big, pos[:], loc[:], blocks1[:], starts1[:])
        cutoff_words(nc, t, a, meta, word, loc)
        send(nc, "keep1", [(meta1, meta), (pos1, pos[:]), (x[:], a["xin"])])
        scatter1 = Scatter(t, "scatter1", meta1, pos1, rec1, REC, a["ea"], filled, n_filled)
        group(nc, c, ps, "by_dst", a["dst"], big, pos[:], loc[:], blocks2[:], starts2[:], beside=scatter1)
        send(nc, "load_meta2", [(word[0], a["ew1"]), (word[1].bitcast(I32), a["src"])])
        with stage(nc, "meta2", "step") as (block, step):
            @block.vector
            def _(dve):
                dve.tensor_copy(meta[:, :, R2_W1], word[0])
                dve.tensor_copy(meta[:, :, R2_SRC].bitcast(I32), word[1].bitcast(I32))
                dve.tensor_copy(meta[:, :, R2_LOC], loc[:])
                dve.memset(meta[:, :, 3], 0.0)
        send(nc, "keep2", [(meta2, meta), (pos2, pos[:])])
    with ExitStack() as ctx:
        first_part(nc, c, Memory(nc, ctx), ps, a, x, h, tmp, rec1, walk1)
    dinv = m.sb("dinv", [P, NB])
    many = m.sb("many", [P, 1], I32)
    C = m.sb("C", [P, NB, NP], BF16)
    with ExitStack() as ctx:
        t = Memory(nc, ctx)
        count_edges(nc, t, ps, rec1, starts1, C, flat_nodes,
                    Scatter(t, "scatter2", meta2, pos2, rec2, 4, None, filled, n_filled))
    with ExitStack() as ctx:
        second_part(nc, c, Memory(nc, ctx), ps, x, h, tmp, rec2, walk2)
    degrees(nc, c, m, ps, C, dinv, many, rec2, walk2, flat_nodes)
    spread = Spread(nc, c, ps, C, dinv, many, rec2, walk2)
    third_part(nc, m, x, h, tmp, spread)
    fourth_part(nc, c, m, ps, a, x, h, tmp, flat_nodes, spread)
    with stage(nc, "result") as (block,):
        @block.sync
        def _(sp):
            sp.dma_start(o["y"], x[:]).then_inc(out_done, 16)
            sp.wait_ge(out_done, 16)


def freqs():
    half = T // 2
    f = np.exp(np.arange(half, dtype=np.float32) * np.float32(-math.log(10000.0) / (half - 1)))
    return np.concatenate([f, f]).astype(np.float32).reshape(T, 1)


def kernel(**inputs):
    import concourse.bacc as bacc
    from concourse.bass_utils import run_bass_kernel_spmd

    v = {k: np.asarray(x) for k, x in inputs.items()}

    def per_edge(x, pad):
        out = np.full((EP,) + x.shape[1:], pad, x.dtype)
        out[:E] = x
        return np.ascontiguousarray(out.reshape(TW, P, *x.shape[1:]).swapaxes(0, 1))

    def per_node(x):
        out = np.zeros((NP,) + x.shape[1:], x.dtype)
        out[:N] = x
        return np.ascontiguousarray(out.reshape(NB, P, *x.shape[1:]).swapaxes(0, 1))

    arrays = {
        "src": per_edge(v["src"], NP), "dst": per_edge(v["dst"], NP), "ea": per_edge(v["edge_attr_40"], 0),
        "ew": per_edge(v["edge_weight"], 0), "ew1": per_edge(v["edge_weight1"][:, 0], 0),
        "xin": per_node(v["x"]), "node_type": per_node(v["node_type_119"]), "node_vec": per_node(v["node_vec"]),
        "freqs": freqs(),
    }
    for k in v:
        if k.startswith(("L0_gnn_", "L3_gnn_")):
            arrays[k[7:]] = np.ascontiguousarray(v[k])

    nc = bacc.Bacc("TRN2", target_bir_lowering=False, num_devices=1)
    a = {k: nc.dram_tensor(k, x.shape, mybir.dt.from_np(x.dtype), kind="ExternalInput").ap() for k, x in arrays.items()}
    o = {"y": nc.dram_tensor("y", (P, NB, H), F32, kind="ExternalOutput").ap()}
    with ExitStack() as ctx:
        network(nc, Memory(nc, ctx), ctx.enter_context(nc.psum_tensor("banks", [P, 8, 512], F32)), a, o)
    r = run_bass_kernel_spmd(nc, [arrays], core_ids=[0])
    y = np.asarray(r.results[0]["y"])
    return y.transpose(1, 0, 2).reshape(NP, H)[:N]
```
